# Optimizing a Trainium2 kernel written in Bass

```python
import numpy as np
import jax
import jax.numpy as jnp

def _softmax(x, axis=-1):
    return jax.nn.softmax(x, axis=axis)

def _gelu(x):
    return jax.nn.gelu(x, approximate=True)

def _silu(x):
    return jax.nn.silu(x)

def _sigmoid(x):
    return jax.nn.sigmoid(x)

def _layernorm(x, axis=-1, eps=1e-05):
    m = jnp.mean(x, axis=axis, keepdims=True)
    v = jnp.var(x, axis=axis, keepdims=True)
    return (x - m) / jnp.sqrt(v + eps)

def _scatter_add(tgt, idx, src, axis=0):
    return tgt.at[idx].add(src)

def _segment_sum(src, seg, n):
    return jax.ops.segment_sum(src, seg, n)
kernel_name = 'mk_xattn_ffn_d1_seqx_r4_c02767'

def setup_inputs(seed: int=0):
    np.random.seed(seed)
    _w = jnp.asarray

    def _rec_inputs():
        import jax
        import jax.numpy as jnp
        _rk = jax.random.key(seed)
        x = 7.22e-05 + 1 * jax.random.normal(jax.random.fold_in(_rk, 1), (8, 256, 512), jnp.float32)
        _lenS = 256 - jax.random.randint(jax.random.fold_in(_rk, 7), (8,), 0, max(1, 256 // 4) + 1, jnp.int32)
        _lenS2 = 256 - jax.random.randint(jax.random.fold_in(_rk, 8), (8,), 0, max(1, 256 // 4) + 1, jnp.int32)
        _ctx_2048P = jax.random.normal(jax.random.fold_in(_rk, 11), (8, 16, 512), jnp.float32)
        _ctx_2048c = jax.random.dirichlet(jax.random.fold_in(_rk, 511), 0.3 * jnp.ones((16,), jnp.float32), (8, 256))
        _ctx_2048t = jnp.einsum('bsk,bkd->bsd', _ctx_2048c, _ctx_2048P)
        _ctx_2048t = _ctx_2048t * jax.lax.rsqrt(jnp.mean(jnp.square(_ctx_2048t)) + 1e-12) * 0.953939
        ctx_2048 = 4.13588e-05 + 0.999923 * (_ctx_2048t + 0.3 * jax.random.normal(jax.random.fold_in(_rk, 611), (8, 256, 512), jnp.float32))
        return (x, ctx_2048)
    x, ctx_2048 = _rec_inputs()

    def _L0_xattn_setup():
        import jax, jax.numpy as jnp
        import numpy as np
        import math
        EMBED = 512
        HEADS = 32
        GROUPS = 8
        GROUP_HEADS = HEADS // GROUPS
        HEAD_DIM = EMBED // HEADS
        B, S = (4, 256)
        key = jax.random.key(seed)
        ks = jax.random.split(key, 8)
        sc = 0.02
        return {'q': jax.random.normal(ks[0], (B, S, EMBED), jnp.float32), 'k': jax.random.normal(ks[1], (B, S, EMBED), jnp.float32), 'v': jax.random.normal(ks[2], (B, S, EMBED), jnp.float32), 'Wq': jax.random.normal(ks[3], (EMBED, EMBED), jnp.float32) * sc, 'Wk': jax.random.normal(ks[4], (GROUPS * HEAD_DIM, EMBED), jnp.float32) * sc, 'Wv': jax.random.normal(ks[5], (GROUPS * HEAD_DIM, EMBED), jnp.float32) * sc, 'Wfc': jax.random.normal(ks[6], (EMBED, EMBED), jnp.float32) * sc, 'bfc': jnp.zeros((EMBED,), jnp.float32)}
    _L0_xattn_all = _L0_xattn_setup()
    _L0_xattn_in = {k: v for k, v in _L0_xattn_all.items() if k in ('Wq', 'Wk', 'Wv', 'Wfc', 'bfc')}
    del _L0_xattn_all

    def _L0_ffn_setup():
        import jax, jax.numpy as jnp
        import numpy as np
        HIDDEN = 512
        NUM_EXPERTS = 32
        TOP_K = 4
        MOE_INTER = 192
        GROUP = 2
        NUM_CHUNK = NUM_EXPERTS // GROUP
        CHUNK_INTER = 128
        SMALL_SCALE = 0.05

        def _routing(x2d, gate_w):
            logits = x2d @ gate_w.T
            rw = jax.nn.softmax(logits.astype(jnp.float32), axis=-1)
            scores = jax.nn.sigmoid(logits.astype(jnp.float32))
            _, sel = jax.lax.top_k(scores, TOP_K)
            w = jnp.take_along_axis(rw, sel, axis=-1)
            w = w / w.sum(axis=-1, keepdims=True)
            return (w.astype(x2d.dtype), sel)

        def _moe(x2d, Wg, Wu, Wd, cw):
            g = jnp.einsum('th,ehi->eti', x2d, Wg)
            u = jnp.einsum('th,ehi->eti', x2d, Wu)
            a = jax.nn.silu(g) * u * cw.T[:, :, None]
            return jnp.einsum('eti,eih->th', a, Wd)
        key = jax.random.key(seed)
        ks = jax.random.split(key, 8)
        s = 0.02
        B, S = (2, 512)
        return {'hidden_states': jax.random.normal(ks[0], (B, S, HIDDEN), jnp.float32), 'gate_w': jax.random.normal(ks[1], (NUM_EXPERTS, HIDDEN), jnp.float32) * s, 'Wg': jax.random.normal(ks[2], (NUM_EXPERTS, HIDDEN, MOE_INTER), jnp.float32) * s, 'Wu': jax.random.normal(ks[3], (NUM_EXPERTS, HIDDEN, MOE_INTER), jnp.float32) * s, 'Wd': jax.random.normal(ks[4], (NUM_EXPERTS, MOE_INTER, HIDDEN), jnp.float32) * s, 'cWg': jax.random.normal(ks[5], (NUM_CHUNK, HIDDEN, CHUNK_INTER), jnp.float32) * s, 'cWu': jax.random.normal(ks[6], (NUM_CHUNK, HIDDEN, CHUNK_INTER), jnp.float32) * s, 'cWd': jax.random.normal(ks[7], (NUM_CHUNK, CHUNK_INTER, HIDDEN), jnp.float32) * s}
    _L0_ffn_all = _L0_ffn_setup()
    _L0_ffn_in = {k: v for k, v in _L0_ffn_all.items() if k in ('gate_w', 'Wg', 'Wu', 'Wd', 'cWg', 'cWu', 'cWd')}
    del _L0_ffn_all
    return {'x': x, 'ctx_2048': ctx_2048, 'L0_xattn_Wq': _L0_xattn_in['Wq'], 'L0_xattn_Wk': _L0_xattn_in['Wk'], 'L0_xattn_Wv': _L0_xattn_in['Wv'], 'L0_xattn_Wfc': _L0_xattn_in['Wfc'], 'L0_xattn_bfc': _L0_xattn_in['bfc'], 'L0_ffn_gate_w': _L0_ffn_in['gate_w'], 'L0_ffn_Wg': _L0_ffn_in['Wg'], 'L0_ffn_Wu': _L0_ffn_in['Wu'], 'L0_ffn_Wd': _L0_ffn_in['Wd'], 'L0_ffn_cWg': _L0_ffn_in['cWg'], 'L0_ffn_cWu': _L0_ffn_in['cWu'], 'L0_ffn_cWd': _L0_ffn_in['cWd']}

def reference(x, ctx_2048, L0_xattn_Wq, L0_xattn_Wk, L0_xattn_Wv, L0_xattn_Wfc, L0_xattn_bfc, L0_ffn_gate_w, L0_ffn_Wg, L0_ffn_Wu, L0_ffn_Wd, L0_ffn_cWg, L0_ffn_cWu, L0_ffn_cWd):
    import jax
    import jax.numpy as jnp

    def _L0_xattn_ref(q, k, v, Wq, Wk, Wv, Wfc, bfc):
        import jax, jax.numpy as jnp
        import numpy as np
        import math
        EMBED = 512
        HEADS = 32
        GROUPS = 8
        GROUP_HEADS = HEADS // GROUPS
        HEAD_DIM = EMBED // HEADS
        B, S = (4, 256)
        N, S_, _ = q.shape
        qh = (q @ Wq.T).reshape(N, S_, HEADS, HEAD_DIM).transpose(0, 2, 1, 3)
        kh = (k @ Wk.T).reshape(N, S_, GROUPS, HEAD_DIM).transpose(0, 2, 1, 3)
        vh = (v @ Wv.T).reshape(N, S_, GROUPS, HEAD_DIM).transpose(0, 2, 1, 3)
        kh = jnp.repeat(kh, GROUP_HEADS, axis=1)
        vh = jnp.repeat(vh, GROUP_HEADS, axis=1)
        score = jnp.einsum('bhqd,bhkd->bhqk', qh, kh) / math.sqrt(HEAD_DIM)
        attn = jax.nn.softmax(score, axis=-1)
        out = jnp.einsum('bhqk,bhkd->bhqd', attn, vh)
        out = out.transpose(0, 2, 1, 3).reshape(N, S_, EMBED)
        return out @ Wfc.T + bfc

    def _L0_ffn_ref(hidden_states, gate_w, Wg, Wu, Wd, cWg, cWu, cWd):
        import jax, jax.numpy as jnp
        import numpy as np
        HIDDEN = 512
        NUM_EXPERTS = 32
        TOP_K = 4
        MOE_INTER = 192
        GROUP = 2
        NUM_CHUNK = NUM_EXPERTS // GROUP
        CHUNK_INTER = 128
        SMALL_SCALE = 0.05

        def _routing(x2d, gate_w):
            logits = x2d @ gate_w.T
            rw = jax.nn.softmax(logits.astype(jnp.float32), axis=-1)
            scores = jax.nn.sigmoid(logits.astype(jnp.float32))
            _, sel = jax.lax.top_k(scores, TOP_K)
            w = jnp.take_along_axis(rw, sel, axis=-1)
            w = w / w.sum(axis=-1, keepdims=True)
            return (w.astype(x2d.dtype), sel)

        def _moe(x2d, Wg, Wu, Wd, cw):
            g = jnp.einsum('th,ehi->eti', x2d, Wg)
            u = jnp.einsum('th,ehi->eti', x2d, Wu)
            a = jax.nn.silu(g) * u * cw.T[:, :, None]
            return jnp.einsum('eti,eih->th', a, Wd)
        B, S, H = hidden_states.shape
        T = B * S
        x = hidden_states.reshape(T, H)
        w, sel = _routing(x, gate_w)
        rows = jnp.arange(T)[:, None]
        cw_large = jnp.zeros((T, NUM_EXPERTS), x.dtype).at[rows, sel].add(w)
        cw_small = jnp.zeros((T, NUM_CHUNK), x.dtype).at[rows, sel // GROUP].add(w)
        large = _moe(x, Wg, Wu, Wd, cw_large)
        small = _moe(x, cWg, cWu, cWd, cw_small)
        return (large + SMALL_SCALE * small).reshape(B, S, H)
    x = x + _L0_xattn_ref(_layernorm(x, axis=-1), ctx_2048, ctx_2048, L0_xattn_Wq, L0_xattn_Wk, L0_xattn_Wv, L0_xattn_Wfc, L0_xattn_bfc)
    x = x + _L0_ffn_ref(_layernorm(x, axis=-1), L0_ffn_gate_w, L0_ffn_Wg, L0_ffn_Wu, L0_ffn_Wd, L0_ffn_cWg, L0_ffn_cWu, L0_ffn_cWd)
    return x

_drawn_inputs = setup_inputs


def setup_inputs(seed=0):
    import zlib

    import numpy as np

    out = dict(_drawn_inputs(seed))
    spreads = {'L0_xattn_bfc': (0.0, 0.1)}
    factors = {'L0_xattn_Wq': 7.487,
     'L0_xattn_Wk': 7.54,
     'L0_ffn_gate_w': 3.922,
     'L0_ffn_Wg': 3.733,
     'L0_ffn_Wu': 3.66,
     'L0_ffn_Wd': 3.648,
     'L0_ffn_cWg': 8.0,
     'L0_ffn_cWu': 8.0,
     'L0_ffn_cWd': 8.0}
    for name, (base, spread) in spreads.items():
        noise = np.random.default_rng([zlib.crc32(name.encode()), seed]).standard_normal(out[name].shape)
        drawn = base * np.exp(spread * noise) if base else spread * noise
        out[name] = jnp.asarray(drawn.astype(out[name].dtype))
    for name, factor in factors.items():
        out[name] = (out[name] * factor).astype(out[name].dtype)
    return out
```

```python
from contextlib import ExitStack

import concourse.bass as bass
from concourse import mybir

ALU = mybir.AluOpType
ACT = mybir.ActivationFunctionType
AX = mybir.AxisListType
F32 = mybir.dt.float32
F32R = mybir.dt.float32r
I32 = mybir.dt.int32
U32 = mybir.dt.uint32
BF16 = mybir.dt.bfloat16

P = 128
D = 512
C = D // P
NB, S = 8, 256
TT = S // P
NT = NB * TT
H, G, DH = 32, 8, 16
J = H // 2
VW = DH + 1
EPS = 1e-5
DMA = 16

ROWS_QK = 3 * DH
ROWS_ST = ROWS_QK + 2


BANK = dict(AV0=0, AV1=1, AV2=0, AV3=1, MT=0, XT0=1, XT1=0, QP0=1, QP1=0, KV=1, OT0=0, FC0=1, OT1=0, FC1=1)


def attention(nc, x_in, ctx_in, wq, wk, wv, wfc, bfc, xs, ident, qd, kd, md):
    with ExitStack() as ctx:
        sb = lambda n, s, d: ctx.enter_context(nc.sbuf_tensor(n, s, d))
        ps = lambda n, s: ctx.enter_context(nc.psum_tensor(n, s, F32))
        sem = lambda n: ctx.enter_context(nc.semaphore(n))

        Wq, Wfc = sb("Wq", [P, C, D], F32), sb("Wfc", [P, C, D], F32)
        Wk, Wv = sb("Wk", [P, C, P], F32), sb("Wv", [P, C, P], F32)
        Bfc = sb("Bfc", [P, D], F32)
        ctxT = [sb(f"ctxT{i}", [P, C, S], F32) for i in range(2)]
        st6 = sb("st6", [P, NT, 6], F32)
        mv = sb("mv", [P, NT, 2], F32)
        eps = sb("eps", [P, 1], F32)
        std, rstd, nmean = sb("std", [P, NT], F32), sb("rstd", [P, NT], F32), sb("nmean", [P, NT], F32)
        xn = sb("xn", [P, TT, D], F32)
        xnT = sb("xnT", [P, C, S], F32)
        qhl = sb("qhl", [P, 2, C * S], F32R)
        khl = sb("khl", [P, 2, S], F32R)
        qst = [sb(f"qst{i}", [P, J, S], F32R) for i in range(2)]
        kst = [sb(f"kst{i}", [P, G, S], F32R) for i in range(2)]
        va = [sb(f"va{i}", [P, TT, G, VW], F32) for i in range(2)]
        mx = sb("mx", [P, TT, 2, J], F32)
        nmh = sb("nmh", [P, TT, H], F32R)
        nm = sb("nm", [P, TT, 2, H], F32)
        mts = sb("mts", [P, P], F32R)
        pt = [sb(f"pt{i}", [P, 2, TT, S], F32) for i in range(2)]
        rec = [sb(f"rec{i}", [P, TT, 8, 1], F32) for i in range(2)]
        o = sb("o", [P, TT, D], F32)
        oT = [sb(f"oT{i}", [P, C, P], F32) for i in range(2)]

        s1 = [ps(f"s1{i}", [P, TT, S]) for i in range(2)]
        stp = [ps(f"stp{i}", [P, 2, TT, S]) for i in range(2)]
        work = [ps(f"work{i}", [P, 512]) for i in range(2)]

        x_loaded, w_loaded, passed = sem("x_loaded"), sem("w_loaded"), sem("passed")
        c_loaded = [sem(f"c_loaded{i}") for i in range(2)]
        ident_ready, set_up = sem("ident_ready"), sem("set_up")
        stats, var_ready, std_ready, rstd_ready = sem("stats"), sem("var_ready"), sem("std_ready"), sem("rstd_ready")
        xn_ready, xb_ready = sem("xn_ready"), sem("xb_ready")
        xt_full, qp_full, kv_full, mt_full = sem("xt_full"), sem("qp_full"), sem("kv_full"), sem("mt_full")
        ot_full, fc_full = sem("ot_full"), sem("fc_full")
        xt_empty, qp_empty, kv_empty, mt_empty = sem("xt_empty"), sem("qp_empty"), sem("kv_empty"), sem("mt_empty")
        av_empty, ot_empty, fc_empty = sem("av_empty"), sem("ot_empty"), sem("fc_empty")
        hi_ready, kl_ready = sem("hi_ready"), sem("kl_ready")
        qk_stored, stack_ready = sem("qk_stored"), sem("stack_ready")
        s1_ready, max_done = sem("s1_ready"), sem("max_done")
        nmh_done, nm_done = sem("nmh_done"), sem("nm_done")
        m_stored, m_ready = sem("m_stored"), sem("m_ready")
        st_ready, exp_done, av_done = sem("st_ready"), sem("exp_done"), sem("av_done")
        rec_done = sem("rec_done")
        bank = lambda name: work[BANK[name]]

        def units(eng, unit):
            with eng.Fori(0, 3) as i:
                unit(0, i * 2)
                unit(1, i * 2)
            unit(6, 0)
            unit(7, 0)

        block = ctx.enter_context(nc.Block())

        @block.sync
        def _(sp):
            xv = x_in.rearrange("(n t p) d -> n p t d", n=4, p=P)
            for n in range(4):
                sp.dma_start(xs[:, 4 * n:4 * n + 4, :], xv[n]).then_inc(x_loaded, DMA)
            sp.dma_start(Wq[:, :, :], wq).then_inc(w_loaded, DMA)
            sp.dma_start(Wk[:, :, :], wk).then_inc(w_loaded, DMA)
            sp.dma_start(Wv[:, :, :], wv).then_inc(w_loaded, DMA)
            sp.dma_start(Wfc[:, :, :], wfc).then_inc(w_loaded, DMA)
            sp.dma_start(Bfc[:, :], bfc).then_inc(w_loaded, DMA)

            def load_ctx(b, par):
                src = ctx_in[bass.ds(b, 1)].rearrange("b p c t -> (b p) c t")
                sp.dma_start(ctxT[par][:, :, :], src).then_inc(c_loaded[par], DMA)

            def stack_qk(b, par):
                sp.wait_ge(qp_empty, b * 2 + 2)
                sp.sem_inc(passed, 1)
                sp.wait_ge(kl_ready, b + 1)
                sp.sem_inc(passed, 1)
                q_b = qd[bass.ds(b, 1)].rearrange("b p l n -> (b p) l n")
                k_b = kd[bass.ds(b, 1)].rearrange("b p l n -> (b p) l n")
                sp.dma_start(q_b, qhl[:, :, :].bitcast(F32)).then_inc(qk_stored, DMA)
                sp.dma_start(k_b, khl[:, :, :].bitcast(F32)).then_inc(qk_stored, DMA)
                sp.wait_ge(qk_stored, b * 2 * DMA + 2 * DMA)
                q_v = qd[bass.ds(b, 1)].rearrange("b (r h d) l n -> (b r) d l h n", r=2, d=DH)
                k_v = kd[bass.ds(b, 1)].rearrange("b (g d) l n -> (b d) l g n", d=DH)
                for r in range(2):
                    for row, l in enumerate((0, 0, 1)):
                        at = 64 * r + DH * row
                        dst = qst[par][at:at + DH, :, :].bitcast(F32).rearrange("d (h c) t -> d h (c t)", c=C)
                        sp.dma_start(dst, q_v[r, :, l]).then_inc(stack_ready, DMA)
                    for row, l in enumerate((0, 1, 0)):
                        at = 64 * r + DH * row
                        sp.dma_start(kst[par][at:at + DH, :, :].bitcast(F32), k_v[:, l]).then_inc(stack_ready, DMA)

            def stack_max(b, par):
                sp.wait_ge(mt_empty, b + 1)
                m_b = md[bass.ds(b, 1)].rearrange("b l r j (t q) -> b t (l r j) q", t=TT)
                m_b = m_b.rearrange("b t n q -> (b t) n q")
                for t in range(TT):
                    sp.dma_start(m_b[t], mts[t * 2 * H:(t + 1) * 2 * H, :].bitcast(F32)).then_inc(m_stored, DMA)
                sp.wait_ge(m_stored, b * 2 * DMA + 2 * DMA)
                m_v = md[bass.ds(b, 1)].rearrange("b l r j t -> (b r) l j t")
                for r in range(2):
                    at = 64 * r + ROWS_QK
                    sp.dma_start(qst[par][at:at + 2, :, :].bitcast(F32), m_v[r]).then_inc(m_ready, DMA)

            load_ctx(0, 0)
            load_ctx(1, 1)
            sp.wait_ge(set_up, 1)
            stack_qk(0, 0)
            stack_max(0, 0)
            stack_qk(1, 1)

            def unit(u, off):
                b = off + u
                if u < 6:
                    load_ctx(b + 2, u % 2)
                if u < 7:
                    stack_max(b + 1, (u + 1) % 2)
                if u < 6:
                    stack_qk(b + 2, u % 2)

            units(sp, unit)

        @block.gpsimd
        def _(pool):
            pool.memset(ident[:, :], 0.0).then_inc(ident_ready, 1)
            pool.wait_ge(ident_ready, 1)
            pool.affine_select(out=ident[:, :], in_=ident[:, :], compare_op=ALU.not_equal, fill=1.0, base=0,
                               pattern=[[-1, P]], channel_multiplier=1).then_inc(ident_ready, 1)
            for i in range(2):
                pool.memset(kst[i][:, :, :].bitcast(F32), 1.0)
                m = pool.memset(va[i][:, :, :, :], 1.0)
            m.then_inc(set_up, 1)
            pool.wait_ge(w_loaded, 5 * DMA)

            with pool.Fori(0, NT) as tile:
                pool.wait_ge(xn_ready, tile + 1)
                xt = xs[:, bass.ds(tile, 1), :].rearrange("p a d -> p (a d)")
                pool.tensor_tensor(xt, xt, Bfc[:, :], ALU.add).then_inc(xb_ready, 1)

        @block.scalar
        def _(act):
            act.wait_ge(var_ready, 1)
            act.activation(std[:, :], mv[:, :, 1], ACT.Sqrt, bias=eps[:, :]).then_inc(std_ready, 1)

            act.sem_inc(ot_empty, 2)
            act.sem_inc(exp_done, 2)

            def project_evac(b):
                for t in range(TT):
                    act.wait_ge(xt_full, b * TT + t + 3)
                    src = bank(f"XT{t}")[:, :].rearrange("p (c t) -> p c t", c=C)
                    act.copy(xnT[:, :, t * P:(t + 1) * P], src).then_inc(xt_empty, 1)
                for n in range(2):
                    act.wait_ge(qp_full, b * 2 + n + 1)
                    act.copy(qhl[:, 0, n * 512:(n + 1) * 512], bank(f"QP{n}")[:, :]).then_inc(hi_ready, 1)
                act.wait_ge(kv_full, b + 1)
                act.copy(khl[:, 0, :], bank("KV")[:, 0:S]).then_inc(hi_ready, 1)

            project_evac(0)
            project_evac(1)

            def unit(u, off):
                b = off + u
                for j in range(J):
                    act.wait_ge(st_ready, b * J + j + 1)
                    act.wait_ge(av_done, b * J + j + 1)
                    act.activation(pt[j % 2][:, :, :, :], stp[j % 2][:, :, :, :], ACT.Exp,
                                   scale=DH ** -0.5).then_inc(exp_done, 1)
                if u < 6:
                    project_evac(b + 2)
                for t in range(TT):
                    act.wait_ge(ot_full, b * TT + t + 1)
                    act.copy(oT[t][:, :, :], bank(f"OT{t}")[:, :].rearrange("p (c t) -> p c t", c=C))\
                       .then_inc(ot_empty, 1)

            units(act, unit)

        @block.vector
        def _(dve):
            dve.sem_inc(max_done, 2)
            dve.sem_inc(fc_empty, 2)
            dve.memset(eps[:, :], EPS)
            for t in range(NT):
                dve.wait_ge(x_loaded, DMA * 4)
                dve.bn_stats(st6[:, t, :], xs[:, t, :]).then_inc(stats, 1)
            for t in range(NT):
                dve.wait_ge(stats, t + 1)
                m = dve.bn_aggr(mv[:, t, :], st6[:, t, :])
            m.then_inc(var_ready, 1)
            dve.wait_ge(std_ready, 1)
            dve.reciprocal(rstd[:, :], std[:, :]).then_inc(rstd_ready, 1)
            dve.wait_ge(rstd_ready, 1)
            dve.wait_ge(var_ready, 1)

            def normalise(b):
                for t in range(TT):
                    tile = b * TT + t
                    dve.wait_ge(xt_full, tile + 1)
                    dve.tensor_scalar(xn[:, t, :], xs[:, bass.ds(tile, 1), :].rearrange("p a d -> p (a d)"),
                                      mv[:, bass.ds(tile, 1), 0], rstd[:, bass.ds(tile, 1)],
                                      ALU.subtract, ALU.mult).then_inc(xn_ready, 1)

            def low_parts(b, par):
                for n in range(2):
                    dve.wait_ge(hi_ready, b * 3 + n + 1)
                    half = slice(n * 512, (n + 1) * 512)
                    dve.tensor_tensor(qhl[:, 1, half], bank(f"QP{n}")[:, :], qhl[:, 0, half].bitcast(F32),
                                      ALU.subtract).then_inc(qp_empty, 1)
                dve.wait_ge(hi_ready, b * 3 + 3)
                dve.tensor_tensor(khl[:, 1, :], bank("KV")[:, 0:S], khl[:, 0, :].bitcast(F32),
                                  ALU.subtract).then_inc(kl_ready, 1)
                dve.wait_ge(set_up, 1)
                dve.tensor_copy(va[par][:, :, :, 0:DH],
                                bank("KV")[:, S:2 * S].rearrange("p (t g d) -> p t g d", t=TT, g=G))\
                   .then_inc(kv_empty, 1)

            def row_max(b, j):
                for r in range(2):
                    dve.wait_ge(s1_ready, b * H + 2 * j + r + 1)
                    dve.tensor_reduce(mx[:, :, r, j:j + 1], s1[r][:, :, :], AX.X, ALU.max).then_inc(max_done, 1)

            def split_max(b):
                dve.wait_ge(max_done, b * H + H + 2)
                m_v = mx[:, :, :, :].rearrange("p t r j -> p t (r j)")
                dve.tensor_scalar(nmh[:, :, :], m_v, -1.0, None, ALU.mult).then_inc(nmh_done, 1)
                dve.wait_ge(nmh_done, b + 1)
                dve.tensor_copy(nm[:, :, 0, :], nmh[:, :, :].bitcast(F32))
                dve.scalar_tensor_tensor(nm[:, :, 1, :], m_v, -1.0, nmh[:, :, :].bitcast(F32), ALU.mult,
                                         ALU.subtract).then_inc(nm_done, 1)

            def max_evac(b):
                dve.wait_ge(mt_full, b + 1)
                dve.tensor_copy(mts[:, :], bank("MT")[:, 0:P]).then_inc(mt_empty, 1)

            def weigh(b, q):
                dve.wait_ge(av_done, b * J + 4 * q + 6)
                v = bank(f"AV{q}")[:, 0:TT * 8 * VW].rearrange("p (t h v) -> p t h v", t=TT, h=8)
                dve.reciprocal(rec[q % 2][:, :, :, :], v[:, :, :, DH:VW]).then_inc(rec_done, 1)
                dve.wait_ge(rec_done, b * 4 + q + 1)
                dst = o[:, :, q * P:(q + 1) * P].rearrange("p t (h d) -> p t h d", h=8)
                dve.tensor_tensor(dst, v[:, :, :, 0:DH], rec[q % 2][:, :, :, :].broadcast_to([P, TT, 8, DH]),
                                  ALU.mult).then_inc(av_empty, 1)

            normalise(0)
            low_parts(0, 0)
            for j in range(J):
                row_max(0, j)
            split_max(0)
            max_evac(0)
            normalise(1)
            low_parts(1, 1)

            def unit(u, off):
                b = off + u
                if u < 6:
                    normalise(b + 2)
                for j in range(J):
                    if u < 7:
                        row_max(b + 1, j)
                    if j % 4 == 1 and j > 4:
                        weigh(b, j // 4 - 1)
                weigh(b, 3)
                if u < 7:
                    split_max(b + 1)
                    max_evac(b + 1)
                if u < 6:
                    low_parts(b + 2, u % 2)
                for t in range(TT):
                    tile = b * TT + t
                    dve.wait_ge(xb_ready, tile + 1)
                    dve.wait_ge(fc_full, tile + 1)
                    xt = xs[:, bass.ds(tile, 1), :].rearrange("p a d -> p (a d)")
                    dve.tensor_tensor(xt, bank(f"FC{t}")[:, :], xt, ALU.add).then_inc(fc_empty, 1)

            units(dve, unit)

        @block.tensor
        def _(pe):
            pe.sem_inc(av_done, 2)
            pe.sem_inc(xt_full, 2)
            pe.wait_ge(ident_ready, 2)
            pe.wait_ge(w_loaded, 5 * DMA)

            def project(b, par):
                for t in range(TT):
                    pe.wait_ge(xn_ready, b * TT + t + 1)
                    if t:
                        free_for_xt1(b)
                    for c in range(C):
                        m = pe.transpose(bank(f"XT{t}")[:, c * P:(c + 1) * P], xn[:, t, c * P:(c + 1) * P],
                                         ident[:, :])
                    m.then_inc(xt_full, 1)
                pe.wait_ge(xt_empty, b * TT + TT)
                for n in range(2):
                    for k in range(2):
                        oc = 2 * n + k
                        for c in range(C):
                            m = pe.matmul(bank(f"QP{n}")[:, k * S:(k + 1) * S], Wq[:, c, oc * P:(oc + 1) * P],
                                          xnT[:, c, :], start=(c == 0), stop=(c == C - 1))
                    m.then_inc(qp_full, 1)
                pe.wait_ge(c_loaded[par], (b - par) * (DMA // 2) + DMA)
                pe.wait_ge(qp_empty, b * 2 + 1)
                w = bank("KV")
                for c in range(C):
                    pe.matmul(w[:, 0:S], Wk[:, c, :], ctxT[par][:, c, :], start=(c == 0), stop=(c == C - 1))
                for t in range(TT):
                    for c in range(C):
                        m = pe.matmul(w[:, S + t * P:S + (t + 1) * P], ctxT[par][:, c, t * P:(t + 1) * P],
                                      Wv[:, c, :], start=(c == 0), stop=(c == C - 1))
                m.then_inc(kv_full, 1)

            def free_for_xt1(b):
                if not (isinstance(b, int) and b == 0):
                    pe.wait_ge(mt_empty, b)

            def scores_for_max(b, par, j):
                if j == 0:
                    pe.wait_ge(stack_ready, b * 12 * DMA + 12 * DMA)
                for r in range(2):
                    pe.wait_ge(max_done, b * H + 2 * j + r + 1)
                    rows = slice(64 * r, 64 * r + ROWS_QK)
                    for t in range(TT):
                        m = pe.matmul(s1[r][:, t, :], qst[par][rows, j, t * P:(t + 1) * P],
                                      kst[par][rows, j // 2, :], start=True, stop=True)
                    m.then_inc(s1_ready, 1)

            def scores(b, par, j):
                if j == 0:
                    pe.wait_ge(m_ready, b * 2 * DMA + 2 * DMA)
                pe.wait_ge(exp_done, b * J + j + 1)
                for r in range(2):
                    rows = slice(64 * r, 64 * r + ROWS_ST)
                    for t in range(TT):
                        m = pe.matmul(stp[j % 2][:, r, t, :], kst[par][rows, j // 2, t * P:(t + 1) * P],
                                      qst[par][rows, j, :], start=True, stop=True)
                m.then_inc(st_ready, 1)

            def values(b, par, j):
                q = j // 4
                if j == 0:
                    pe.wait_ge(ot_empty, b * TT + 2)
                elif j == 4:
                    pe.wait_ge(fc_empty, b * TT + 2)
                elif j % 4 == 0:
                    pe.wait_ge(av_empty, b * 4 + q - 1)
                w = bank(f"AV{q}")[:, 0:TT * 8 * VW].rearrange("p (t h v) -> p t h v", t=TT, h=8)
                pe.wait_ge(exp_done, b * J + j + 3)
                for r in range(2):
                    for t in range(TT):
                        for k in range(TT):
                            m = pe.matmul(w[:, t, 2 * (j % 4) + r, :], pt[j % 2][:, r, k, t * P:(t + 1) * P],
                                          va[par][:, k, j // 2, :], start=(k == 0), stop=(k == TT - 1))
                m.then_inc(av_done, 1)

            def transpose_max(b):
                pe.wait_ge(nm_done, b + 1)
                pe.transpose(bank("MT")[:, 0:P], nm[:, :, :, :].rearrange("p t l h -> p (t l h)"),
                             ident[:, :]).then_inc(mt_full, 1)

            def project_out(b):
                pe.wait_ge(av_empty, b * 4 + 4)
                for t in range(TT):
                    if t:
                        pe.wait_ge(ot_empty, b * TT + t + 2)
                    for c in range(C):
                        m = pe.transpose(bank(f"OT{t}")[:, c * P:(c + 1) * P], o[:, t, c * P:(c + 1) * P],
                                         ident[:, :])
                    m.then_inc(ot_full, 1)
                    if t:
                        pe.wait_ge(fc_empty, b * TT + t + 2)
                    pe.wait_ge(ot_empty, b * TT + t + 3)
                    for c in range(C):
                        m = pe.matmul(bank(f"FC{t}")[:, :], oT[t][:, c, :], Wfc[:, c, :], start=(c == 0),
                                      stop=(c == C - 1))
                    m.then_inc(fc_full, 1)

            project(0, 0)
            for j in range(J):
                scores_for_max(0, 0, j)
            pe.wait_ge(qp_empty, 2)
            transpose_max(0)
            pe.wait_ge(kv_empty, 1)
            project(1, 1)
            pe.wait_ge(qp_empty, 4)
            pe.wait_ge(kv_empty, 2)

            def unit(u, off):
                b = off + u
                for j in range(J):
                    if u < 7:
                        scores_for_max(b + 1, (u + 1) % 2, j)
                    scores(b, u % 2, j)
                    if j:
                        values(b, u % 2, j - 1)
                values(b, u % 2, J - 1)
                if u < 7:
                    pe.wait_ge(av_empty, b * 4 + 3)
                    transpose_max(b + 1)
                if u < 6:
                    pe.wait_ge(av_empty, b * 4 + 4)
                    project(b + 2, u % 2)
                    pe.wait_ge(qp_empty, b * 2 + 6)
                    pe.wait_ge(kv_empty, b + 3)
                elif u == 6:
                    pe.wait_ge(mt_empty, b + 2)
                project_out(b)

            units(pe, unit)


E_, K_ = 32, 4
TILE = P
NS = (NT * P * K_) // TILE + E_
IL, IS = 192, 128
IW = IL + IS
SMALL = 0.05
NW = 2


def route(nc, gate_w, xs, ident, xd, tabs):
    w4, dest, tok, slot_e, slot_buf, cum_i = tabs
    with ExitStack() as ctx:
        sb = lambda n, s, d: ctx.enter_context(nc.sbuf_tensor(n, s, d))
        ps = lambda n, s: ctx.enter_context(nc.psum_tensor(n, s, F32))
        sem = lambda n: ctx.enter_context(nc.semaphore(n))

        gw = sb("gw", [P, C, E_], F32)
        st6, mv = sb("r_st6", [P, NT, 6], F32), sb("r_mv", [P, NT, 2], F32)
        eps, std, rstd = sb("r_eps", [P, 1], F32), sb("r_std", [P, NT], F32), sb("r_rstd", [P, NT], F32)
        xn = [sb(f"r_xn{i}", [P, D], F32) for i in range(2)]
        xnT = [sb(f"r_xnT{i}", [P, C, P], F32) for i in range(2)]
        lg = sb("lg", [P, NT, E_], F32)
        top, idx = sb("top", [P, NT, 8], F32), sb("idx", [P, NT, 8], U32)
        d4, e4 = sb("d4", [P, NT, K_], F32), sb("e4", [P, NT, K_], F32)
        s4, r4 = sb("s4", [P, NT, 1], F32), sb("r4", [P, NT, 1], F32)
        idf = sb("idf", [P, NT, K_], F32)
        iota_e = sb("iota_e", [P, E_], F32)
        iota_j = sb("iota_j", [P, NT - 1], F32)
        iota_s = sb("iota_s", [P, NS], F32)
        iota_r = sb("iota_r", [P, P], BF16)
        iota_q = sb("iota_q", [P, NS], BF16)
        row = sb("row", [P, 1], F32)
        tcol = sb("tcol", [P, NT], F32)
        oh = sb("oh", [P, NT, K_, E_], F32)
        pr = sb("pr", [P, NT, K_, E_], F32)
        m1, m2 = sb("m1", [P, NT, E_], F32), sb("m2", [P, NT, E_], F32)
        mask = sb("mask", [P, NT, E_], BF16)
        upper = sb("upper", [P, P], BF16)
        ones = sb("ones", [P, P], BF16)
        cmp_n = sb("cmp_n", [P, E_, NT - 1], F32)
        n_e = sb("n_e", [P, E_], F32)
        sl, cum, base, zero = (sb(n, [P, E_], F32) for n in ("sl", "cum", "base", "zero"))
        pos = sb("pos", [P, NT, E_], F32)
        destf = sb("destf", [P, NT, K_], F32)
        qi, ri = sb("qi", [P, NT, K_], I32), sb("ri", [P, NT, K_], I32)
        qf, rf = sb("qf", [P, NT * K_], F32), sb("rf", [P, NT * K_], F32)
        desti = sb("desti", [P, NT, K_], I32)
        cmp_s = sb("cmp_s", [P, NS, E_], F32)
        sef = sb("sef", [P, NS], F32)
        ohr = [sb(f"ohr{k}", [P, P], BF16) for k in range(K_)]
        ohq = [sb(f"ohq{k}", [P, 2, NS], BF16) for k in range(K_)]
        tabf = sb("tabf", [P, NS], F32)

        xt_ps = [ps(f"r_xt{i}", [P, 512]) for i in range(2)]
        lg_ps = [ps(f"r_lg{i}", [P, 512]) for i in range(2)]
        pos_ps, cnt_ps, tab_ps = ps("pos_ps", [P, NT, E_]), ps("cnt_ps", [P, 512]), ps("tab_ps", [P, 512])

        gw_loaded, iotas, tri = sem("gw_loaded"), sem("iotas"), sem("tri")
        step = sem("r_step")
        var_ready, std_ready = sem("r_var"), sem("r_std_ready")
        xn_ready, xn_stored = sem("r_xn"), [sem(f"r_stored{i}") for i in range(2)]
        xt_full, xt_empty, lg_full, lg_empty = sem("r_xtf"), sem("r_xte"), sem("r_lgf"), sem("r_lge")
        d4_ready, e4_ready = sem("d4_ready"), sem("e4_ready")
        mask_ready, pos_full, tabs_in, tab_used, tab_full = (sem(n) for n in (
            "mask_ready", "pos_full", "tabs_in", "tab_used", "tab_full"))

        block = ctx.enter_context(nc.Block())

        @block.sync
        def _(sp):
            sp.dma_start(gw[:, :, :], gate_w).then_inc(gw_loaded, DMA)
            with sp.Fori(0, NT // 2) as i:
                for p in range(2):
                    t = i * 2 + p
                    sp.wait_ge(xn_ready, t + 1)
                    sp.dma_start(xd[bass.ds(t * P, P), :], xn[p][:, :]).then_inc(xn_stored[p], DMA)
            for p in range(2):
                sp.wait_ge(xn_stored[p], DMA * (NT // 2 + 1))

        @block.gpsimd
        def _(pool):
            pool.sem_inc(xn_stored[0], DMA)
            pool.sem_inc(xn_stored[1], DMA)
            pool.iota(iota_e[:, :], [[1, E_]], 0, 0, allow_small_or_imprecise_dtypes=True)
            pool.iota(iota_j[:, :], [[P, NT - 1]], P, 0, allow_small_or_imprecise_dtypes=True)
            pool.iota(iota_s[:, :], [[1, NS]], 0, 0, allow_small_or_imprecise_dtypes=True)
            pool.iota(iota_r[:, :], [[1, P]], 0, 0, allow_small_or_imprecise_dtypes=True)
            pool.iota(iota_q[:, :], [[1, NS]], 0, 0, allow_small_or_imprecise_dtypes=True)
            pool.iota(row[:, :], [[0, 1]], 0, 1, allow_small_or_imprecise_dtypes=True)
            pool.iota(tcol[:, :], [[1, NT]], 0, 0, allow_small_or_imprecise_dtypes=True)
            pool.memset(zero[:, :], 0.0)
            pool.memset(ones[:, :], 1.0)
            pool.memset(upper[:, :], 1.0).then_inc(iotas, 1)
            pool.wait_ge(iotas, 1)
            pool.affine_select(out=upper[:, :], in_=upper[:, :], compare_op=ALU.is_gt, fill=0.0, base=0,
                               pattern=[[1, P]], channel_multiplier=-1).then_inc(tri, 1)

        @block.scalar
        def _(act):
            act.wait_ge(var_ready, 1)
            act.activation(std[:, :], mv[:, :, 1], ACT.Sqrt, bias=eps[:, :]).then_inc(std_ready, 1)
            with act.Fori(0, NT // 2) as i:
                for p in range(2):
                    t = i * 2 + p
                    act.wait_ge(xt_full, t + 3)
                    act.copy(xnT[p][:, :, :], xt_ps[p][:, :].rearrange("p (c t) -> p c t", c=C)).then_inc(xt_empty, 1)
            act.wait_ge(d4_ready, 1)
            act.activation(e4[:, :, :], d4[:, :, :], ACT.Exp).then_inc(e4_ready, 1)

        @block.tensor
        def _(pe):
            pe.sem_inc(xt_full, 2)
            pe.wait_ge(gw_loaded, DMA)
            with pe.Fori(0, NT // 2) as i:
                for p in range(2):
                    t = i * 2 + p
                    pe.wait_ge(xn_ready, t + 1)
                    for c in range(C):
                        m = pe.transpose(xt_ps[p][:, c * P:(c + 1) * P], xn[p][:, c * P:(c + 1) * P], ident[:, :])
                    m.then_inc(xt_full, 1)
                    pe.wait_ge(xt_empty, t + 1)
                    pe.wait_ge(lg_empty, t + 1)
                    for c in range(C):
                        m = pe.matmul(lg_ps[p][:, 0:E_], xnT[p][:, c, :], gw[:, c, :], start=(c == 0),
                                      stop=(c == C - 1))
                    m.then_inc(lg_full, 1)
            pe.wait_ge(tri, 1)
            pe.wait_ge(mask_ready, 1)
            pe.matmul(pos_ps[:, :, :], upper[:, :], mask[:, :, :], start=True, stop=True)
            for t in range(NT - 1):
                m = pe.matmul(pos_ps[:, t + 1:NT, :], ones[:, :],
                              mask[:, t:t + 1, :].broadcast_to([P, NT - 1 - t, E_]),
                              start=False, stop=True, skip_group_check=True)
            for t in range(NT):
                m = pe.matmul(cnt_ps[:, 0:E_], ones[:, :], mask[:, t, :], start=(t == 0), stop=(t == NT - 1))
            m.then_inc(pos_full, 1)
            with pe.Fori(0, NT) as t:
                for k in range(K_):
                    pe.wait_ge(tabs_in, t * K_ + k + 1)
                    pe.matmul(tab_ps[:, 0:2 * NS], ohr[k][:, :], ohq[k][:, :, :].rearrange("p a n -> p (a n)"),
                              start=False, stop=True, skip_group_check=True).then_inc(tab_used, 1)

        @block.vector
        def _(dve):
            made = [0]

            def done(ins):
                made[0] += 1
                ins.then_inc(step, 1)
                dve.wait_ge(step, made[0])

            dve.sem_inc(lg_empty, 2)
            dve.sem_inc(tab_used, K_)
            dve.memset(eps[:, :], EPS)
            for t in range(NT):
                s = dve.bn_stats(st6[:, t, :], xs[:, t, :])
            done(s)
            for t in range(NT):
                s = dve.bn_aggr(mv[:, t, :], st6[:, t, :])
            s.then_inc(var_ready, 1)
            dve.wait_ge(std_ready, 1)
            done(dve.reciprocal(rstd[:, :], std[:, :]))

            def normalise(t, p):
                dve.wait_ge(xt_full, t + 1)
                dve.wait_ge(xn_stored[p], (t - p) * (DMA // 2) + DMA)
                dve.tensor_scalar(xn[p][:, :], xs[:, bass.ds(t, 1), :].rearrange("p a d -> p (a d)"),
                                  mv[:, bass.ds(t, 1), 0], rstd[:, bass.ds(t, 1)], ALU.subtract,
                                  ALU.mult).then_inc(xn_ready, 1)

            def logits(t, p):
                dve.wait_ge(lg_full, t + 1)
                dve.tensor_copy(lg[:, bass.ds(t, 1), :].rearrange("p a e -> p (a e)"),
                                lg_ps[p][:, 0:E_]).then_inc(lg_empty, 1)

            normalise(0, 0)
            with dve.Fori(0, NT // 2 - 1) as i:
                for p in range(2):
                    normalise(i * 2 + p + 1, (p + 1) % 2)
                    logits(i * 2 + p, p)
            normalise(NT - 1, 1)
            logits(NT - 2, 0)
            logits(NT - 1, 1)
            dve.wait_ge(lg_empty, NT + 2)
            for t in range(NT):
                s = dve.max(top[:, t, :], lg[:, t, :])
            done(s)
            for t in range(NT):
                s = dve.max_index(idx[:, t, :], top[:, t, :], lg[:, t, :])
            done(s)
            dve.tensor_tensor(d4[:, :, :], top[:, :, 0:K_], top[:, :, 0:1].broadcast_to([P, NT, K_]),
                              ALU.subtract).then_inc(d4_ready, 1)
            done(dve.tensor_copy(idf[:, :, :], idx[:, :, 0:K_]))
            dve.wait_ge(iotas, 1)
            ie = iota_e[:, :].unsqueeze(1).broadcast_to([P, NT, E_])
            for k in range(K_):
                s = dve.tensor_tensor(oh[:, :, k, :], ie, idf[:, :, k:k + 1].broadcast_to([P, NT, E_]), ALU.is_equal)
            done(s)
            dve.tensor_tensor(m1[:, :, :], oh[:, :, 0, :], oh[:, :, 1, :], ALU.add)
            done(dve.tensor_tensor(m2[:, :, :], oh[:, :, 2, :], oh[:, :, 3, :], ALU.add))
            dve.tensor_tensor(mask[:, :, :], m1[:, :, :], m2[:, :, :], ALU.add).then_inc(mask_ready, 1)
            dve.wait_ge(e4_ready, 1)
            done(dve.tensor_reduce(s4[:, :, :], e4[:, :, :], AX.X, ALU.add))
            done(dve.reciprocal(r4[:, :, :], s4[:, :, :]))
            dve.tensor_tensor(w4[:, :, :], e4[:, :, :], r4[:, :, :].broadcast_to([P, NT, K_]), ALU.mult)
            dve.wait_ge(pos_full, 1)
            done(dve.tensor_copy(n_e[:, :], cnt_ps[:, 0:E_]))
            done(dve.tensor_tensor(cmp_n[:, :, :], n_e[:, :].unsqueeze(2).broadcast_to([P, E_, NT - 1]),
                                   iota_j[:, :].unsqueeze(1).broadcast_to([P, E_, NT - 1]), ALU.is_gt))
            done(dve.tensor_reduce(sl[:, :], cmp_n[:, :, :], AX.X, ALU.add))
            done(dve.tensor_scalar(sl[:, :], sl[:, :], 1.0, None, ALU.add))
            done(dve.tensor_tensor_scan(cum[:, :], sl[:, :], zero[:, :], 0.0, ALU.add, ALU.add))
            done(dve.tensor_tensor(base[:, :], cum[:, :], sl[:, :], ALU.subtract))
            done(dve.tensor_scalar(base[:, :], base[:, :], float(TILE), None, ALU.mult))
            dve.tensor_copy(cum_i[:, :], cum[:, :])
            done(dve.tensor_tensor(pos[:, :, :], pos_ps[:, :, :], base[:, :].unsqueeze(1).broadcast_to([P, NT, E_]),
                                   ALU.add))
            for k in range(K_):
                s = dve.tensor_tensor(pr[:, :, k, :], oh[:, :, k, :], pos[:, :, :], ALU.mult)
            done(s)
            done(dve.tensor_reduce(destf[:, :, :], pr[:, :, :, :], AX.X, ALU.add))
            dve.tensor_copy(dest[:, :, :], destf[:, :, :])
            done(dve.tensor_copy(desti[:, :, :], destf[:, :, :]))
            dve.tensor_scalar(qi[:, :, :], desti[:, :, :], 7, None, ALU.arith_shift_right)
            done(dve.tensor_scalar(ri[:, :, :], desti[:, :, :], P - 1, None, ALU.bitwise_and))
            dve.tensor_copy(qf[:, :], qi[:, :, :].rearrange("p t k -> p (t k)"))
            dve.tensor_copy(rf[:, :], ri[:, :, :].rearrange("p t k -> p (t k)"))
            done(dve.tensor_tensor(cmp_s[:, :, :], iota_s[:, :].unsqueeze(2).broadcast_to([P, NS, E_]),
                                   cum[:, :].unsqueeze(1).broadcast_to([P, NS, E_]), ALU.is_ge))
            done(dve.tensor_reduce(sef[:, :], cmp_s[:, :, :], AX.X, ALU.add))
            done(dve.tensor_scalar(sef[:, :], sef[:, :], float(E_ - 1), None, ALU.min))
            done(dve.tensor_copy(slot_e[:, :], sef[:, :]))
            dve.tensor_scalar(slot_buf[:, :], slot_e[:, :], NW - 1, None, ALU.bitwise_and)
            done(dve.memset(tab_ps[:, 0:2 * NS], 0.0))
            with dve.Fori(0, NT) as t:
                for k in range(K_):
                    dve.wait_ge(tab_used, t * K_ + k + 1)
                    q1, r1 = qf[:, bass.ds(t * K_ + k, 1)], rf[:, bass.ds(t * K_ + k, 1)]
                    dve.tensor_scalar(ohr[k][:, :], iota_r[:, :], r1, None, ALU.is_equal)
                    dve.tensor_scalar(ohq[k][:, 0, :], iota_q[:, :], q1, row[:, :], ALU.is_equal, ALU.mult)
                    dve.tensor_scalar(ohq[k][:, 1, :], iota_q[:, :], q1, tcol[:, bass.ds(t, 1)], ALU.is_equal,
                                      ALU.mult).then_inc(tabs_in, 1)
            dve.wait_ge(tab_used, NT * K_ + K_)
            done(dve.tensor_copy(tabf[:, :], tab_ps[:, 0:NS]))
            done(dve.scalar_tensor_tensor(tabf[:, :], tab_ps[:, NS:2 * NS], float(P), tabf[:, :], ALU.mult, ALU.add))
            done(dve.tensor_copy(tok[:, :], tabf[:, :]))


def experts(nc, wgu_l, wgu_s, wd_l, wd_s, xs, ident, xd, yd, tabs, out):
    w4, dest, tok, slot_e, slot_buf, cum_i = tabs
    with ExitStack() as ctx:
        sb = lambda n, s, d: ctx.enter_context(nc.sbuf_tensor(n, s, d))
        ps = lambda n, s: ctx.enter_context(nc.psum_tensor(n, s, F32))
        sem = lambda n: ctx.enter_context(nc.semaphore(n))

        GU = sb("GU", [P, NW, C, 2, IW], F32)
        DW = sb("DW", [P, NW, 3, D], F32)
        idx = [sb(f"gidx{i}", [P, 1], U32) for i in range(2)]
        xg = [sb(f"xg{i}", [P, D], F32) for i in range(2)]
        xT = [sb(f"xT{i}", [P, C, P], F32) for i in range(2)]
        sg = [sb(f"sg{i}", [P, IW], F32) for i in range(2)]
        a = [sb(f"a{i}", [P, IW], F32) for i in range(2)]
        aT = [sb(f"aT{i}", [P, 3, P], F32) for i in range(2)]
        yb = [sb(f"yb{i}", [P, D], F32) for i in range(2)]
        yidx = [sb(f"yidx{i}", [P, K_], U32) for i in range(2)]
        yg = [sb(f"yg{i}", [P, K_, D], F32) for i in range(2)]

        xt_ps = [ps(f"xt_ps{i}", [P, 512]) for i in range(2)]
        g_ps = [ps(f"g_ps{i}", [P, 512]) for i in range(2)]
        u_ps = [ps(f"u_ps{i}", [P, 512]) for i in range(2)]
        at_ps, y_ps = ps("at_ps", [P, 4, P]), ps("y_ps", [P, D])

        w_loaded = [sem(f"w_loaded{i}") for i in range(NW)]
        experts_ready, slots_done = sem("experts_ready"), sem("slots_done")
        idx_ready, x_loaded = sem("idx_ready"), [sem(f"xg_loaded{i}") for i in range(2)]
        xt_full, xt_empty, gu_full = sem("xt_full2"), sem("xt_empty2"), sem("gu_full")
        sg_ready, a_ready, at_full, at_empty = sem("sg_ready"), sem("a_ready"), sem("at_full"), sem("at_empty")
        y_empty, y_stored = sem("y_empty"), [sem(f"y_stored{i}") for i in range(2)]
        yi_ready, yg_loaded = sem("yi_ready"), [sem(f"yg_loaded{i}") for i in range(2)]
        passed = sem("e_passed")
        yg_used, added, out_stored = sem("yg_used"), sem("added"), sem("out_stored")

        block = ctx.enter_context(nc.Block())

        @block.sync
        def _(sp):
            def load(i, p):
                e = i * 2 + p
                gl = wgu_l[bass.ds(e, 1)].rearrange("e p n f -> (e p) n f")
                gs = wgu_s[bass.ds(i, 1)].rearrange("e p n f -> (e p) n f")
                dst = GU[:, p].rearrange("p c g f -> p (c g) f")
                sp.dma_start(dst[:, :, 0:IL], gl).then_inc(w_loaded[p], DMA)
                sp.dma_start(dst[:, :, IL:IW], gs).then_inc(w_loaded[p], DMA)
                dl = wd_l[bass.ds(e, 1)].rearrange("e r d -> (e r) d")
                ds = wd_s[bass.ds(i, 1)].rearrange("e r d -> (e r) d")
                sp.dma_start(DW[:, p, 0, :], dl[0:P, :]).then_inc(w_loaded[p], DMA)
                sp.dma_start(DW[0:IL - P, p, 1, :], dl[P:IL, :]).then_inc(w_loaded[p], DMA)
                sp.dma_start(DW[:, p, 2, :], ds).then_inc(w_loaded[p], DMA)

            def arrived(i, p):
                sp.wait_ge(w_loaded[p], i * 5 * DMA + 5 * DMA)
                sp.sem_inc(experts_ready, 1)

            load(0, 0)
            load(0, 1)
            arrived(0, 0)
            arrived(0, 1)
            with sp.Fori(1, E_ // 2) as i:
                for p in range(2):
                    last = sp.value_load(cum_i[0:1, bass.ds(i * 2 + p - 2, 1)], min_val=1, max_val=NS)
                    sp.wait_ge(slots_done, last)
                    load(i, p)
                    arrived(i, p)
            with sp.Fori(0, NT) as t:
                sp.wait_ge(added, t * K_ + K_)
                sp.dma_start(out[bass.ds(t * P, P), :],
                             xs[:, bass.ds(t, 1), :].rearrange("p a d -> p (a d)")).then_inc(out_stored, DMA)
            sp.wait_ge(out_stored, NT * DMA)

        @block.gpsimd
        def _(pool):
            with pool.Fori(0, NS // 2) as i:
                for p in range(2):
                    s = i * 2 + p
                    pool.wait_ge(xt_full, s + 1)
                    pool.tensor_copy(idx[p][:, :], tok[:, bass.ds(s, 1)]).then_inc(idx_ready, 1)
                    pool.wait_ge(idx_ready, s + 1)
                    pool.sem_inc(passed, 1)
                    pool.indirect_dma_start(xg[p][:, :], None, xd[:, :], bass.IndirectOffsetOnAxis(idx[p][:, :], 0))\
                        .then_inc(x_loaded[p], DMA)
            for p in range(2):
                pool.wait_ge(y_stored[p], DMA * (NS // 2 + 1))
            with pool.Fori(0, NT // 2) as i:
                for p in range(2):
                    t = i * 2 + p
                    pool.wait_ge(yg_used, t + 1)
                    pool.tensor_copy(yidx[p][:, :], dest[:, bass.ds(t, 1), :].rearrange("p a k -> p (a k)"))\
                        .then_inc(yi_ready, 1)
                    pool.wait_ge(yi_ready, t + 1)
                    pool.sem_inc(passed, 1)
                    for k in range(K_):
                        pool.indirect_dma_start(yg[p][:, k, :], None, yd[:, :],
                                                bass.IndirectOffsetOnAxis(yidx[p][:, k:k + 1], 0))\
                            .then_inc(yg_loaded[p], DMA)

        def slots(eng, first, body, last):
            first()
            with eng.Fori(1, NS // 2 - 1) as i:
                body(i * 2, 0)
                body(i * 2 + 1, 1)
            last()

        @block.scalar
        def _(act):
            act.sem_inc(y_stored[0], DMA)
            act.sem_inc(y_stored[1], DMA)

            def x_evac(s, p):
                act.wait_ge(xt_full, s + 3)
                act.copy(xT[p][:, :, :], xt_ps[p][:, :].rearrange("p (c t) -> p c t", c=C)).then_inc(xt_empty, 1)

            def silu(s, p):
                act.wait_ge(gu_full, s + 1)
                act.activation(sg[p][:, :], g_ps[p][:, 0:IW], ACT.Silu).then_inc(sg_ready, 1)

            def y_evac(s, p):
                act.wait_ge(slots_done, s + 1)
                act.wait_ge(y_stored[p], (s - p) * (DMA // 2) + DMA)
                act.copy(yb[p][:, :], y_ps[:, :]).then_inc(y_empty, 1)
                act.wait_ge(y_empty, s + 1)
                act.dma_start(yd[bass.ds(s * TILE, TILE), :], yb[p][:, :]).then_inc(y_stored[p], DMA)

            def slot(s, p, first=False, last=False):
                if not last:
                    x_evac(s + 1, 1 - p)
                silu(s, p)
                if not first:
                    y_evac(s - 1, 1 - p)

            x_evac(0, 0)
            slot(0, 0, first=True)
            slot(1, 1)
            with act.Fori(1, NS // 2 - 1) as i:
                slot(i * 2, 0)
                slot(i * 2 + 1, 1)
            slot(NS - 2, 0)
            slot(NS - 1, 1, last=True)
            y_evac(NS - 1, 1)

        @block.vector
        def _(dve):
            def at_evac(s, p):
                dve.wait_ge(at_full, s + 1)
                dve.tensor_copy(aT[p][:, 0::2, :], at_ps[:, 0:3:2, :])
                dve.tensor_copy(aT[p][0:IL - P, 1, :], at_ps[0:IL - P, 1, :]).then_inc(at_empty, 1)

            def gated(s, p):
                dve.wait_ge(sg_ready, s + 1)
                dve.tensor_tensor(a[p][:, 0:IL], u_ps[p][:, 0:IL], sg[p][:, 0:IL], ALU.mult)
                dve.scalar_tensor_tensor(a[p][:, IL:IW], u_ps[p][:, IL:IW], SMALL, sg[p][:, IL:IW], ALU.mult,
                                         ALU.mult).then_inc(a_ready, 1)

            gated(0, 0)
            at_evac(0, 0)
            gated(1, 1)
            with dve.Fori(1, NS // 2) as i:
                for p in range(2):
                    at_evac(i * 2 + p - 1, 1 - p)
                    gated(i * 2 + p, p)
            at_evac(NS - 1, 1)
            dve.sem_inc(yg_used, 2)
            with dve.Fori(0, NT // 2) as i:
                for p in range(2):
                    t = i * 2 + p
                    dve.wait_ge(yg_loaded[p], i * K_ * DMA + K_ * DMA)
                    xt = xs[:, bass.ds(t, 1), :].rearrange("p a d -> p (a d)")
                    for k in range(K_):
                        w = w4[:, bass.ds(t, 1), k]
                        ins = dve.scalar_tensor_tensor(xt, yg[p][:, k, :], w, xt, ALU.mult, ALU.add)
                        ins.then_inc(added, 1)
                        dve.wait_ge(added, t * K_ + k + 1)
                    dve.sem_inc(yg_used, 1)

        @block.tensor
        def _(pe):
            pe.sem_inc(xt_full, 2)

            def transpose_x(s, p):
                if p is not None:
                    pe.wait_ge(x_loaded[p], (s - p) * (DMA // 2) + DMA)
                for c in range(C):
                    m = pe.transpose(xt_ps[p][:, c * P:(c + 1) * P], xg[p][:, c * P:(c + 1) * P], ident[:, :])
                m.then_inc(xt_full, 1)

            def gate_up(s, p, buf):
                pe.wait_ge(xt_empty, s + 1)
                for ps_, g in ((g_ps, 0), (u_ps, 1)):
                    for c in range(C):
                        m = pe.matmul(ps_[p][:, 0:IW], xT[p][:, c, :],
                                      GU[:, bass.ds(buf, 1), c, g, :].rearrange("p a f -> p (a f)"),
                                      start=(c == 0), stop=(c == C - 1))
                m.then_inc(gu_full, 1)

            def transpose_a(s, p):
                pe.wait_ge(a_ready, s + 1)
                pe.transpose(at_ps[:, 0, :], a[p][:, 0:P], ident[:, :])
                pe.transpose(at_ps[0:IL - P, 1, :], a[p][:, P:IL], ident[:, :])
                pe.transpose(at_ps[:, 2, :], a[p][:, IL:IW], ident[:, :]).then_inc(at_full, 1)

            def down(s, p, buf):
                pe.wait_ge(at_empty, s + 1)
                if not (isinstance(s, int) and s == 0):
                    pe.wait_ge(y_empty, s)
                for c in range(3):
                    rows = slice(0, IL - P) if c == 1 else slice(0, P)
                    m = pe.matmul(y_ps[:, :], aT[p][rows, c, :],
                                  DW[rows, bass.ds(buf, 1), c, :].rearrange("p a d -> p (a d)"),
                                  start=(c == 0), stop=(c == 2))
                m.then_inc(slots_done, 1)

            def slot(s, p, first=False, last=False):
                e = pe.value_load(slot_e[0:1, bass.ds(s, 1)], min_val=0, max_val=E_ - 1)
                buf = pe.value_load(slot_buf[0:1, bass.ds(s, 1)], min_val=0, max_val=NW - 1)
                if not first:
                    transpose_a(s - 1, 1 - p)
                if not last:
                    transpose_x(s + 1, 1 - p)
                pe.wait_ge(experts_ready, e + 1)
                gate_up(s, p, buf)
                if not first:
                    down(s - 1, 1 - p, pe.value_load(slot_buf[0:1, bass.ds(s - 1, 1)], min_val=0, max_val=NW - 1))

            transpose_x(0, 0)
            slot(0, 0, first=True)
            slot(1, 1)
            with pe.Fori(1, NS // 2 - 1) as i:
                slot(i * 2, 0)
                slot(i * 2 + 1, 1)
            slot(NS - 2, 0)
            slot(NS - 1, 1, last=True)
            transpose_a(NS - 1, 1)
            down(NS - 1, 1, pe.value_load(slot_buf[0:1, bass.ds(NS - 1, 1)], min_val=0, max_val=NW - 1))


def build(nc, t, out):
    qd = nc.dram_tensor("qd", (NB, P, 2, C * S), F32, kind="Internal").ap()
    kd = nc.dram_tensor("kd", (NB, P, 2, S), F32, kind="Internal").ap()
    md = nc.dram_tensor("md", (NB, 2, 2, J, S), F32, kind="Internal").ap()
    xd = nc.dram_tensor("xd", (NT * P, D), F32, kind="Internal").ap()
    yd = nc.dram_tensor("yd", (NS * TILE, D), F32, kind="Internal").ap()
    with ExitStack() as ctx:
        sb = lambda n, s, d: ctx.enter_context(nc.sbuf_tensor(n, s, d))
        xs, ident = sb("xs", [P, NT, D], F32), sb("ident", [P, P], F32)
        tabs = (sb("w4", [P, NT, K_], F32), sb("dest", [P, NT, K_], U32), sb("tok", [P, NS], U32),
                sb("slot_e", [P, NS], I32), sb("slot_buf", [P, NS], I32), sb("cum_i", [P, E_], I32))
        attention(nc, t["x"], t["ctx"], t["wq"], t["wk"], t["wv"], t["wfc"], t["bfc"], xs, ident, qd, kd, md)
        route(nc, t["gate_w"], xs, ident, xd, tabs)
        experts(nc, t["wgu_l"], t["wgu_s"], t["wd_l"], t["wd_s"], xs, ident, xd, yd, tabs, out)


def kernel(**inputs):
    import numpy as np
    import concourse.bacc as bacc
    from concourse.bass_utils import run_bass_kernel_spmd

    a = {k: np.asarray(v) for k, v in inputs.items()}
    order = np.arange(D).reshape(C, C, 2, DH).transpose(1, 2, 0, 3).reshape(-1)

    def rows_in(w):
        return w.reshape(C, P, -1).transpose(1, 0, 2)

    def gate_up(g, u):
        n, _, f = g.shape
        return np.stack([g, u], 1).reshape(n, 2, C, P, f).transpose(0, 3, 2, 1, 4).reshape(n, P, 2 * C, f)

    arrays = {
        "x": a["x"].reshape(NT * P, D),
        "ctx": a["ctx_2048"].transpose(0, 2, 1).reshape(NB, C, P, S).transpose(0, 2, 1, 3),
        "wq": rows_in(a["L0_xattn_Wq"].T[:, order]),
        "wk": rows_in(a["L0_xattn_Wk"].T),
        "wv": rows_in(a["L0_xattn_Wv"].T),
        "wfc": rows_in(a["L0_xattn_Wfc"].T),
        "bfc": np.broadcast_to(a["L0_xattn_bfc"], (P, D)),
        "gate_w": rows_in(a["L0_ffn_gate_w"].T),
        "wgu_l": gate_up(a["L0_ffn_Wg"], a["L0_ffn_Wu"]),
        "wgu_s": gate_up(a["L0_ffn_cWg"], a["L0_ffn_cWu"]),
        "wd_l": a["L0_ffn_Wd"],
        "wd_s": a["L0_ffn_cWd"],
    }
    arrays = {f"in_{k}": np.ascontiguousarray(v) for k, v in arrays.items()}
    nc = bacc.Bacc("TRN2", target_bir_lowering=False, num_devices=1)
    t = {k[3:]: nc.dram_tensor(k, v.shape, F32, kind="ExternalInput").ap() for k, v in arrays.items()}
    out = nc.dram_tensor("out_x", (NT * P, D), F32, kind="ExternalOutput").ap()
    build(nc, t, out)
    r = run_bass_kernel_spmd(nc, [arrays], core_ids=[0])
    return r.results[0]["out_x"].reshape(NB, S, D)
```

```python
from contextlib import ExitStack

import concourse.bass as bass
from concourse import mybir

ALU = mybir.AluOpType
ACT = mybir.ActivationFunctionType
AX = mybir.AxisListType
F32 = mybir.dt.float32
I32 = mybir.dt.int32
U32 = mybir.dt.uint32
BF16 = mybir.dt.bfloat16
F16 = mybir.dt.float16

P = 128
D = 512
C = D // P
NB, S = 8, 256
TT = S // P
NT = NB * TT
H, G, DH = 32, 8, 16
J = H // 2
EPS = 1e-5
DMA = 16

Q_PART = (0, 0, 0, 1, 1, 2)
K_PART = (0, 1, 2, 0, 1, 0)
ROWS_QK = DH * len(Q_PART)
ROWS_ST = ROWS_QK + 3
NP = 4
LAG = 3
QLAG = 4
GAIN = 15


def due(j):
    upto = lambda n: max(0, n * J // (J - QLAG))
    return range(upto(j - QLAG), upto(j + 1 - QLAG))


def attention(nc, x_in, ctx_in, wq, wk, wv, wfc, bfc, xs, ident, qd, kd, md):
    with ExitStack() as ctx:
        sb = lambda n, s, d: ctx.enter_context(nc.sbuf_tensor(n, s, d))
        ps = lambda n, s: ctx.enter_context(nc.psum_tensor(n, s, F32))
        sem = lambda n: ctx.enter_context(nc.semaphore(n))

        Wq, Wfc = sb("Wq", [P, C, D], F32), sb("Wfc", [P, C, D], F32)
        Wk, Wv = sb("Wk", [P, C, P], F32), sb("Wv", [P, C, P], F32)
        Bfc = sb("Bfc", [P, D], F32)
        identb = sb("identb", [P, P], BF16)
        ctxT = [sb(f"ctxT{i}", [P, C, S], F32) for i in range(2)]
        st6 = sb("st6", [P, NT, 6], F32)
        mv = sb("mv", [P, NT, 2], F32)
        eps, gain = sb("eps", [P, 1], F32), sb("gain", [P, 1], F32)
        std, rstd = sb("std", [P, NT], F32), sb("rstd", [P, NT], F32)
        xn = sb("xn", [P, TT, D], F32)
        xnT = sb("xnT", [P, C, S], F32)
        q3 = sb("q3", [P, 3, C * S], BF16)
        kv = [sb(f"kv{i}", [P, 4, 2 * S], BF16) for i in range(2)]
        res = [sb(f"res{i}", [P, 2 * S], F32) for i in range(3)]
        qst = [sb(f"qst{i}", [P, H, S], BF16) for i in range(2)]
        kst = [sb(f"kst{i}", [P, G, S], BF16) for i in range(2)]
        mx = sb("mx", [P, TT, H], F32)
        mres = sb("mres", [P, TT, H], F32)
        nm = sb("nm", [P, TT, 3, H], BF16)
        mts = sb("mts", [3 * H, S], BF16)
        pt = [sb(f"pt{i}", [P, 2, TT, S], F32) for i in range(2)]
        ph = [sb(f"ph{i}", [P, 2, TT, S], F16) for i in range(NP)]
        pl = [sb(f"pl{i}", [P, 2, TT, S], F16) for i in range(NP)]
        rec = [sb(f"rec{i}", [P, TT * C, 1], F32) for i in range(2)]
        av = [sb(f"av{i}", [P, TT * C, DH], F32) for i in range(2)]
        o = sb("o", [P, TT, D], F32)
        oT = [sb(f"oT{i}", [P, C, P], F32) for i in range(2)]

        s1 = [ps(f"s1{i}", [P, TT, S]) for i in range(2)]
        stp = [ps(f"stp{i}", [P, 2, TT, S]) for i in range(2)]
        work = [ps(f"work{i}", [P, 512]) for i in range(2)]
        flat = lambda bank: bank[:, :, :].rearrange("p t s -> p (t s)")
        mt_bank = flat(s1[0]).bitcast(BF16)[0:3 * H, 0:S]
        XT, QP, KV = (flat(s1[1]), flat(s1[0])), (flat(s1[1]), flat(s1[0])), flat(s1[1])
        OT, FC = work[0], work[1]

        w_loaded, passed = sem("w_loaded"), sem("passed")
        x_loaded = [sem(f"x_loaded{n}") for n in range(4)]
        c_loaded = [sem(f"c_loaded{i}") for i in range(2)]
        ident_ready, set_up = sem("ident_ready"), sem("set_up")
        stats, var_ready, std_ready, rstd_ready = sem("stats"), sem("var_ready"), sem("std_ready"), sem("rstd_ready")
        xn_ready, xb_ready = sem("xn_ready"), sem("xb_ready")
        xt_full, qp_full, kv_full, mt_full = sem("xt_full"), sem("qp_full"), sem("kv_full"), sem("mt_full")
        ot_full, fc_full = sem("ot_full"), sem("fc_full")
        xt_empty, pr_empty, mt_empty = sem("xt_empty"), sem("pr_empty"), sem("mt_empty")
        av_empty, ot_empty, fc_empty = sem("av_empty"), sem("ot_empty"), sem("fc_empty")
        hi_ready, mid_ready, lo_ready = sem("hi_ready"), sem("mid_ready"), sem("lo_ready")
        qk_stored, stack_ready = sem("qk_stored"), sem("stack_ready")
        s1_ready, max_done = sem("s1_ready"), sem("max_done")
        nm_step, nm_done = sem("nm_step"), sem("nm_done")
        m_stored, m_ready = sem("m_stored"), sem("m_ready")
        st_ready, ph_done, exp_done, pl_done, av_done = (
            sem("st_ready"), sem("ph_done"), sem("exp_done"), sem("pl_done"), sem("av_done"))
        rec_done, sum_done = sem("rec_done"), sem("sum_done")

        def parts(par, n):
            if n == 2:
                return [kv[par][:, l, :] for l in range(3)]
            return [q3[:, l, n * 512:(n + 1) * 512] for l in range(3)]

        def units(eng, unit):
            with eng.Fori(0, 3) as i:
                unit(0, i * 2)
                unit(1, i * 2)
            unit(6, 0)
            unit(7, 0)

        block = ctx.enter_context(nc.Block())

        @block.sync
        def _(sp):
            xv = x_in.rearrange("(n t p) d -> n p t d", n=4, p=P)
            sp.dma_start(xs[:, 0:4, :], xv[0]).then_inc(x_loaded[0], DMA)
            sp.dma_start(Wq[:, :, :], wq).then_inc(w_loaded, DMA)

            def load_ctx(b, par):
                src = ctx_in[bass.ds(b, 1)].rearrange("b p c t -> (b p) c t")
                sp.dma_start(ctxT[par][:, :, :], src).then_inc(c_loaded[par], DMA)

            sp.dma_start(Wk[:, :, :], wk).then_inc(w_loaded, DMA)
            sp.dma_start(Wv[:, :, :], wv).then_inc(w_loaded, DMA)
            load_ctx(0, 0)
            for n in range(1, 4):
                sp.dma_start(xs[:, 4 * n:4 * n + 4, :], xv[n]).then_inc(x_loaded[n], DMA)
            load_ctx(1, 1)
            sp.dma_start(Wfc[:, :, :], wfc).then_inc(w_loaded, DMA)
            sp.dma_start(Bfc[:, :], bfc).then_inc(w_loaded, DMA)

            def stack_qk(b, par):
                sp.wait_ge(lo_ready, b * 3 + 6)
                sp.sem_inc(passed, 1)
                q_b = qd[bass.ds(b, 1)].rearrange("b p l n -> (b p) l n")
                k_b = kd[bass.ds(b, 1)].rearrange("b p l n -> (b p) l n")
                sp.dma_start(q_b, q3[:, :, :]).then_inc(qk_stored, DMA)
                sp.dma_start(k_b, kv[par][:, 0:3, 0:S]).then_inc(qk_stored, DMA)
                sp.wait_ge(qk_stored, b * 2 * DMA + 2 * DMA)
                q_v = qd[bass.ds(b, 1)].rearrange("b (g d) l n -> (b l) d g n", d=DH)
                k_v = kd[bass.ds(b, 1)].rearrange("b (g d) l n -> (b l) d g n", d=DH)
                for row, (ql, kl) in enumerate(zip(Q_PART, K_PART)):
                    rows = slice(DH * row, DH * row + DH)
                    dst = qst[par][rows, :, :].rearrange("d (g c) t -> d g (c t)", c=C)
                    sp.dma_start(dst, q_v[ql]).then_inc(stack_ready, DMA)
                    sp.dma_start(kst[par][rows, :, :], k_v[kl]).then_inc(stack_ready, DMA)

            def stack_max(b, par):
                sp.wait_ge(mt_empty, b + 1)
                sp.dma_start(md[bass.ds(b, 1)].rearrange("b l h s -> (b l h) s"), mts[:, :]).then_inc(m_stored, DMA)
                sp.wait_ge(m_stored, b * DMA + DMA)
                sp.dma_start(qst[par][ROWS_QK:ROWS_ST, :, :], md[bass.ds(b, 1)].rearrange("b l h s -> (b l) h s"))\
                  .then_inc(m_ready, DMA)

            sp.wait_ge(set_up, 1)
            stack_qk(0, 0)
            stack_max(0, 0)
            stack_qk(1, 1)

            def unit(u, off):
                b = off + u
                if u < 6:
                    load_ctx(b + 2, u % 2)
                if u < 7:
                    stack_max(b + 1, (u + 1) % 2)
                if u < 6:
                    stack_qk(b + 2, u % 2)

            units(sp, unit)

        @block.gpsimd
        def _(pool):
            pool.memset(ident[:, :], 0.0).then_inc(ident_ready, 1)
            pool.memset(identb[:, :], 0.0).then_inc(ident_ready, 1)
            pool.wait_ge(ident_ready, 2)
            for eye in (ident, identb):
                pool.affine_select(out=eye[:, :], in_=eye[:, :], compare_op=ALU.not_equal, fill=1.0, base=0,
                                   pattern=[[-1, P]], channel_multiplier=1).then_inc(ident_ready, 1)
            for i in range(2):
                pool.memset(kst[i][:, :, :], 1.0)
                m = pool.memset(kv[i][:, 3, :], 1.0)
            m.then_inc(set_up, 1)
            pool.wait_ge(w_loaded, 5 * DMA)
            pool.sem_inc(pl_done, 2)
            pool.sem_inc(lo_ready, 3)

            def add_bias(b):
                for t in range(TT):
                    tile = b * TT + t
                    pool.wait_ge(xn_ready, tile + 1)
                    xt = xs[:, bass.ds(tile, 1), :].rearrange("p a d -> p (a d)")
                    pool.tensor_tensor(xt, xt, Bfc[:, :], ALU.add).then_inc(xb_ready, 1)

            def low_part(b, par, n):
                pool.wait_ge(mid_ready, b * 3 + n + 1)
                two, three = parts(par, n)[1:]
                pool.tensor_tensor(three, res[n][:, :], two, ALU.subtract).then_inc(lo_ready, 1)

            for b in range(2):
                for n in range(3):
                    low_part(b, b, n)
                add_bias(b)

            def unit(u, off):
                b = off + u
                for j in range(J):
                    pool.wait_ge(exp_done, b * J + j + 3)
                    pool.tensor_tensor(pl[j % NP][:, :, :, :], pt[j % 2][:, :, :, :], ph[j % NP][:, :, :, :],
                                       ALU.subtract).then_inc(pl_done, 1)
                if u < 6:
                    add_bias(b + 2)
                    for n in range(3):
                        low_part(b + 2, u % 2, n)

            units(pool, unit)

        @block.scalar
        def _(act):
            def deviations(k):
                act.wait_ge(var_ready, k + 1)
                act.activation(std[:, 4 * k:4 * k + 4], mv[:, 4 * k:4 * k + 4, 1], ACT.Sqrt,
                               bias=eps[:, :]).then_inc(std_ready, 1)

            act.sem_inc(ot_empty, 1)
            act.sem_inc(exp_done, 2)

            def project_evac(b, par):
                for t in range(TT):
                    act.wait_ge(xt_full, b * TT + t + 3)
                    src = XT[t].rearrange("p (c t) -> p c t", c=C)
                    act.copy(xnT[:, :, t * P:(t + 1) * P], src).then_inc(xt_empty, 1)
                if not (isinstance(b, int) and b == 0):
                    act.wait_ge(qk_stored, b * 2 * DMA)
                for n in range(2):
                    act.wait_ge(qp_full, b * 2 + n + 1)
                    act.copy(parts(par, n)[0], QP[n]).then_inc(hi_ready, 1)
                for n in range(2):
                    act.wait_ge(pr_empty, b * 3 + n + 1)
                    act.copy(parts(par, n)[1], res[n][:, :]).then_inc(mid_ready, 1)
                act.wait_ge(kv_full, b + 1)
                act.copy(parts(par, 2)[0], KV).then_inc(hi_ready, 1)
                act.wait_ge(pr_empty, b * 3 + 3)
                act.copy(parts(par, 2)[1], res[2][:, :]).then_inc(mid_ready, 1)

            deviations(0)
            project_evac(0, 0)
            project_evac(1, 1)
            for k in range(1, 4):
                deviations(k)

            def unit(u, off):
                b = off + u
                for j in range(J):
                    act.wait_ge(st_ready, b * J + j + 1)
                    act.wait_ge(av_done, b * J + j + 1)
                    act.activation(ph[j % NP][:, :, :, :], stp[j % 2][:, :, :, :], ACT.Exp, bias=gain[:, :],
                                   scale=DH ** -0.5).then_inc(ph_done, 1)
                    act.wait_ge(pl_done, b * J + j + 1)
                    act.activation(pt[j % 2][:, :, :, :], stp[j % 2][:, :, :, :], ACT.Exp, bias=gain[:, :],
                                   scale=DH ** -0.5).then_inc(exp_done, 1)
                if u < 6:
                    project_evac(b + 2, u % 2)
                for t in range(TT):
                    act.wait_ge(ot_full, b * TT + t + 1)
                    act.copy(oT[t][:, :, :], OT[:, :].rearrange("p (c t) -> p c t", c=C)).then_inc(ot_empty, 1)

            units(act, unit)

        @block.vector
        def _(dve):
            dve.sem_inc(max_done, 2)
            dve.sem_inc(fc_empty, 1)
            dve.memset(eps[:, :], EPS)
            dve.memset(gain[:, :], GAIN * 0.6931471805599453)

            def statistics(k):
                dve.wait_ge(x_loaded[k], DMA)
                for t in range(4 * k, 4 * k + 4):
                    dve.bn_stats(st6[:, t, :], xs[:, t, :]).then_inc(stats, 1)
                for t in range(4 * k, 4 * k + 4):
                    dve.wait_ge(stats, t + 1)
                    m = dve.bn_aggr(mv[:, t, :], st6[:, t, :])
                m.then_inc(var_ready, 1)
                dve.wait_ge(std_ready, k + 1)
                dve.reciprocal(rstd[:, 4 * k:4 * k + 4], std[:, 4 * k:4 * k + 4]).then_inc(rstd_ready, 1)
                dve.wait_ge(rstd_ready, k + 1)

            def normalise(b):
                for t in range(TT):
                    tile = b * TT + t
                    dve.wait_ge(xt_full, tile + 1)
                    dve.tensor_scalar(xn[:, t, :], xs[:, bass.ds(tile, 1), :].rearrange("p a d -> p (a d)"),
                                      mv[:, bass.ds(tile, 1), 0], rstd[:, bass.ds(tile, 1)],
                                      ALU.subtract, ALU.mult).then_inc(xn_ready, 1)

            def residue(b, par, n):
                dve.wait_ge(hi_ready, b * 3 + n + 1)
                dve.wait_ge(lo_ready, b * 3 + n + 1)
                dve.tensor_tensor(res[n][:, :], KV if n == 2 else QP[n], parts(par, n)[0],
                                  ALU.subtract).then_inc(pr_empty, 1)

            def row_max(b, j):
                for r in range(2):
                    dve.wait_ge(s1_ready, b * H + 2 * j + r + 1)
                    dve.tensor_reduce(mx[:, :, 2 * j + r:2 * j + r + 1], s1[r][:, :, :], AX.X, ALU.max)\
                       .then_inc(max_done, 1)

            def split_max(b):
                dve.wait_ge(max_done, b * H + H + 2)
                dve.tensor_scalar(nm[:, :, 0, :], mx[:, :, :], -1.0, None, ALU.mult).then_inc(nm_step, 1)
                dve.wait_ge(nm_step, b * 3 + 1)
                dve.scalar_tensor_tensor(mres[:, :, :], mx[:, :, :], -1.0, nm[:, :, 0, :], ALU.mult,
                                         ALU.subtract).then_inc(nm_step, 1)
                dve.wait_ge(nm_step, b * 3 + 2)
                dve.tensor_copy(nm[:, :, 1, :], mres[:, :, :]).then_inc(nm_step, 1)
                dve.wait_ge(nm_step, b * 3 + 3)
                dve.tensor_tensor(nm[:, :, 2, :], mres[:, :, :], nm[:, :, 1, :], ALU.subtract).then_inc(nm_done, 1)

            def max_evac(b):
                dve.wait_ge(mt_full, b + 1)
                dve.tensor_copy(mts[:, :], mt_bank).then_inc(mt_empty, 1)

            def weigh(b, g):
                dve.wait_ge(av_done, b * J + 2 * g + 2 + NP)
                v = work[g % 2][:, :].rearrange("p (h l d) -> p h l d", l=4, d=DH)
                dve.reciprocal(rec[g % 2][:, :, :], v[:, :, 3, 0:1]).then_inc(rec_done, 1)
                dve.tensor_reduce(av[g % 2][:, :, :].unsqueeze(3), v[:, :, 0:3, :].rearrange("p h l d -> p h d l"),
                                  AX.X, ALU.add).then_inc(sum_done, 1)
                dve.wait_ge(rec_done, b * G + g + 1)
                dve.wait_ge(sum_done, b * G + g + 1)
                dst = o[:, :, g * 64:(g + 1) * 64].rearrange("p t (h d) -> p t h d", h=C)
                dve.tensor_tensor(dst, av[g % 2][:, :, :].rearrange("p (t h) d -> p t h d", t=TT),
                                  rec[g % 2][:, :, :].rearrange("p (t h) d -> p t h d", t=TT)
                                  .broadcast_to([P, TT, C, DH]), ALU.mult).then_inc(av_empty, 1)

            statistics(0)
            normalise(0)
            normalise(1)
            for b in range(2):
                for n in range(3):
                    residue(b, b, n)
            for k in range(1, 4):
                statistics(k)
            for j in range(J):
                row_max(0, j)
            split_max(0)
            max_evac(0)

            def unit(u, off):
                b = off + u
                if u < 6:
                    normalise(b + 2)
                for j in range(J):
                    if u < 7:
                        for m in due(j):
                            row_max(b + 1, m)
                    if j % 2 and j >= 5:
                        weigh(b, (j - 5) // 2)
                if u < 7:
                    split_max(b + 1)
                    max_evac(b + 1)
                weigh(b, 6)
                if u < 6:
                    residue(b + 2, u % 2, 0)
                    residue(b + 2, u % 2, 1)
                weigh(b, 7)
                if u < 6:
                    residue(b + 2, u % 2, 2)
                for t in range(TT):
                    tile = b * TT + t
                    dve.wait_ge(xb_ready, tile + 1)
                    dve.wait_ge(fc_full, tile + 1)
                    xt = xs[:, bass.ds(tile, 1), :].rearrange("p a d -> p (a d)")
                    dve.tensor_tensor(xt, FC[:, :], xt, ALU.add).then_inc(fc_empty, 1)

            units(dve, unit)

        @block.tensor
        def _(pe):
            pe.sem_inc(av_done, NP)
            pe.sem_inc(xt_full, 2)
            pe.wait_ge(ident_ready, 4)
            pe.wait_ge(w_loaded, 5 * DMA)

            def transpose_x(b):
                for t in range(TT):
                    pe.wait_ge(xn_ready, b * TT + t + 1)
                    if t and not (isinstance(b, int) and b < 2):
                        pe.wait_ge(mt_empty, b)
                    for c in range(C):
                        m = pe.transpose(XT[t][:, c * P:(c + 1) * P], xn[:, t, c * P:(c + 1) * P], ident[:, :])
                    m.then_inc(xt_full, 1)

            def project_q(b):
                pe.wait_ge(xt_empty, b * TT + TT)
                for n in range(2):
                    for k in range(2):
                        oc = 2 * n + k
                        for c in range(C):
                            m = pe.matmul(QP[n][:, k * S:(k + 1) * S], Wq[:, c, oc * P:(oc + 1) * P],
                                          xnT[:, c, :], start=(c == 0), stop=(c == C - 1))
                    m.then_inc(qp_full, 1)

            def project_kv(b, par):
                pe.wait_ge(c_loaded[par], (b - par) * (DMA // 2) + DMA)
                pe.wait_ge(pr_empty, b * 3 + 1)
                for c in range(C):
                    pe.matmul(KV[:, 0:S], Wk[:, c, :], ctxT[par][:, c, :], start=(c == 0), stop=(c == C - 1))
                for t in range(TT):
                    for c in range(C):
                        m = pe.matmul(KV[:, S + t * P:S + (t + 1) * P], ctxT[par][:, c, t * P:(t + 1) * P],
                                      Wv[:, c, :], start=(c == 0), stop=(c == C - 1))
                m.then_inc(kv_full, 1)

            def scores_for_max(b, par, j):
                if j == 0:
                    pe.wait_ge(stack_ready, b * 12 * DMA + 12 * DMA)
                for r in range(2):
                    pe.wait_ge(max_done, b * H + 2 * j + r + 1)
                    for t in range(TT):
                        m = pe.matmul(s1[r][:, t, :], qst[par][0:ROWS_QK, 2 * j + r, t * P:(t + 1) * P],
                                      kst[par][0:ROWS_QK, j // 2, :], start=True, stop=True)
                    m.then_inc(s1_ready, 1)

            def scores(b, par, j):
                if j == 0:
                    pe.wait_ge(m_ready, b * DMA + DMA)
                pe.wait_ge(exp_done, b * J + j + 1)
                for r in range(2):
                    for t in range(TT):
                        m = pe.matmul(stp[j % 2][:, r, t, :], kst[par][0:ROWS_ST, j // 2, t * P:(t + 1) * P],
                                      qst[par][0:ROWS_ST, 2 * j + r, :], start=True, stop=True)
                m.then_inc(st_ready, 1)

            def values(b, par, j):
                g = j // 2
                if j == 0:
                    pe.wait_ge(ot_empty, b * TT + 1)
                elif j == 2:
                    pe.wait_ge(fc_empty, b * TT + 1)
                elif j % 2 == 0:
                    pe.wait_ge(av_empty, b * G + g - 1)
                w = work[g % 2][:, :].rearrange("p (t h l d) -> p t h l d", t=TT, h=C, l=4)
                pe.wait_ge(pl_done, b * J + j + 3)
                for r in range(2):
                    for t in range(TT):
                        for k in range(TT):
                            for part in (ph, pl):
                                m = pe.matmul(w[:, t, 2 * (j % 2) + r], part[j % NP][:, r, k, t * P:(t + 1) * P],
                                              kv[par][:, :, S + k * P + g * DH:S + k * P + (g + 1) * DH],
                                              start=(k == 0 and part is ph), stop=(k == TT - 1 and part is pl))
                m.then_inc(av_done, 1)

            def transpose_max(b):
                pe.wait_ge(nm_done, b + 1)
                for t in range(TT):
                    m = pe.transpose(mt_bank[:, t * P:(t + 1) * P], nm[:, t].rearrange("p l h -> p (l h)"),
                                     identb[:, :])
                m.then_inc(mt_full, 1)

            def project_out(b):
                pe.wait_ge(av_empty, b * G + G)
                for t in range(TT):
                    if t:
                        pe.wait_ge(ot_empty, b * TT + t + 1)
                    for c in range(C):
                        m = pe.transpose(OT[:, c * P:(c + 1) * P], o[:, t, c * P:(c + 1) * P], ident[:, :])
                    m.then_inc(ot_full, 1)
                    if t:
                        pe.wait_ge(fc_empty, b * TT + t + 1)
                    pe.wait_ge(ot_empty, b * TT + t + 2)
                    for c in range(C):
                        m = pe.matmul(FC[:, :], oT[t][:, c, :], Wfc[:, c, :], start=(c == 0), stop=(c == C - 1))
                    m.then_inc(fc_full, 1)

            for b in range(2):
                if b:
                    pe.wait_ge(pr_empty, 3)
                transpose_x(b)
                project_q(b)
                project_kv(b, b)
            pe.wait_ge(pr_empty, 6)
            for j in range(J):
                scores_for_max(0, 0, j)
            transpose_max(0)
            pe.wait_ge(mt_empty, 1)

            def unit(u, off):
                b = off + u
                for j in range(J):
                    scores(b, u % 2, j)
                    if u < 7:
                        for m in due(j):
                            scores_for_max(b + 1, (u + 1) % 2, m)
                    if j >= LAG:
                        values(b, u % 2, j - LAG)
                if u < 7:
                    transpose_max(b + 1)
                values(b, u % 2, J - 3)
                if u < 6:
                    transpose_x(b + 2)
                values(b, u % 2, J - 2)
                if u < 6:
                    project_q(b + 2)
                values(b, u % 2, J - 1)
                if u < 6:
                    project_kv(b + 2, u % 2)
                project_out(b)

            units(pe, unit)


E_, K_ = 32, 4
TILE = P
NS = (NT * P * K_) // TILE + E_
IL, IS = 192, 128
IW = IL + IS
SMALL = 0.05
NW = 2


def route(nc, gate_w, xs, ident, xd, tabs):
    w4, dest, tok, slot_e, slot_buf, cum_i = tabs
    with ExitStack() as ctx:
        sb = lambda n, s, d: ctx.enter_context(nc.sbuf_tensor(n, s, d))
        ps = lambda n, s: ctx.enter_context(nc.psum_tensor(n, s, F32))
        sem = lambda n: ctx.enter_context(nc.semaphore(n))

        gw = sb("gw", [P, C, E_], F32)
        st6, mv = sb("r_st6", [P, NT, 6], F32), sb("r_mv", [P, NT, 2], F32)
        eps, std, rstd = sb("r_eps", [P, 1], F32), sb("r_std", [P, NT], F32), sb("r_rstd", [P, NT], F32)
        xn = [sb(f"r_xn{i}", [P, D], F32) for i in range(2)]
        xnT = [sb(f"r_xnT{i}", [P, C, P], F32) for i in range(2)]
        lg = sb("lg", [P, NT, E_], F32)
        top, idx = sb("top", [P, NT, 8], F32), sb("idx", [P, NT, 8], U32)
        d4, e4 = sb("d4", [P, NT, K_], F32), sb("e4", [P, NT, K_], F32)
        s4, r4 = sb("s4", [P, NT, 1], F32), sb("r4", [P, NT, 1], F32)
        idf = sb("idf", [P, NT, K_], F32)
        iota_e = sb("iota_e", [P, E_], F32)
        iota_j = sb("iota_j", [P, NT - 1], F32)
        iota_s = sb("iota_s", [P, NS], F32)
        iota_r = sb("iota_r", [P, P], BF16)
        iota_q = sb("iota_q", [P, NS], BF16)
        row = sb("row", [P, 1], F32)
        tcol = sb("tcol", [P, NT], F32)
        oh = sb("oh", [P, NT, K_, E_], F32)
        pr = sb("pr", [P, NT, K_, E_], F32)
        m1, m2 = sb("m1", [P, NT, E_], F32), sb("m2", [P, NT, E_], F32)
        mask = sb("mask", [P, NT, E_], BF16)
        upper = sb("upper", [P, P], BF16)
        ones = sb("ones", [P, P], BF16)
        cmp_n = sb("cmp_n", [P, E_, NT - 1], F32)
        n_e = sb("n_e", [P, E_], F32)
        sl, cum, base, zero = (sb(n, [P, E_], F32) for n in ("sl", "cum", "base", "zero"))
        pos = sb("pos", [P, NT, E_], F32)
        destf = sb("destf", [P, NT, K_], F32)
        qi, ri = sb("qi", [P, NT, K_], I32), sb("ri", [P, NT, K_], I32)
        qf, rf = sb("qf", [P, NT * K_], F32), sb("rf", [P, NT * K_], F32)
        desti = sb("desti", [P, NT, K_], I32)
        cmp_s = sb("cmp_s", [P, NS, E_], F32)
        sef = sb("sef", [P, NS], F32)
        ohr = [sb(f"ohr{k}", [P, P], BF16) for k in range(K_)]
        ohq = [sb(f"ohq{k}", [P, 2, NS], BF16) for k in range(K_)]
        tabf = sb("tabf", [P, NS], F32)

        xt_ps = [ps(f"r_xt{i}", [P, 512]) for i in range(2)]
        lg_ps = [ps(f"r_lg{i}", [P, 512]) for i in range(2)]
        pos_ps, cnt_ps, tab_ps = ps("pos_ps", [P, NT, E_]), ps("cnt_ps", [P, 512]), ps("tab_ps", [P, 512])

        gw_loaded, iotas, tri = sem("gw_loaded"), sem("iotas"), sem("tri")
        step = sem("r_step")
        var_ready, std_ready = sem("r_var"), sem("r_std_ready")
        xn_ready, xn_stored = sem("r_xn"), [sem(f"r_stored{i}") for i in range(2)]
        xt_full, xt_empty, lg_full, lg_empty = sem("r_xtf"), sem("r_xte"), sem("r_lgf"), sem("r_lge")
        d4_ready, e4_ready = sem("d4_ready"), sem("e4_ready")
        mask_ready, pos_full, tabs_in, tab_used, tab_full = (sem(n) for n in (
            "mask_ready", "pos_full", "tabs_in", "tab_used", "tab_full"))

        block = ctx.enter_context(nc.Block())

        @block.sync
        def _(sp):
            sp.dma_start(gw[:, :, :], gate_w).then_inc(gw_loaded, DMA)
            with sp.Fori(0, NT // 2) as i:
                for p in range(2):
                    t = i * 2 + p
                    sp.wait_ge(xn_ready, t + 1)
                    sp.dma_start(xd[bass.ds(t * P, P), :], xn[p][:, :]).then_inc(xn_stored[p], DMA)
            for p in range(2):
                sp.wait_ge(xn_stored[p], DMA * (NT // 2 + 1))

        @block.gpsimd
        def _(pool):
            pool.sem_inc(xn_stored[0], DMA)
            pool.sem_inc(xn_stored[1], DMA)
            pool.iota(iota_e[:, :], [[1, E_]], 0, 0, allow_small_or_imprecise_dtypes=True)
            pool.iota(iota_j[:, :], [[P, NT - 1]], P, 0, allow_small_or_imprecise_dtypes=True)
            pool.iota(iota_s[:, :], [[1, NS]], 0, 0, allow_small_or_imprecise_dtypes=True)
            pool.iota(iota_r[:, :], [[1, P]], 0, 0, allow_small_or_imprecise_dtypes=True)
            pool.iota(iota_q[:, :], [[1, NS]], 0, 0, allow_small_or_imprecise_dtypes=True)
            pool.iota(row[:, :], [[0, 1]], 0, 1, allow_small_or_imprecise_dtypes=True)
            pool.iota(tcol[:, :], [[1, NT]], 0, 0, allow_small_or_imprecise_dtypes=True)
            pool.memset(zero[:, :], 0.0)
            pool.memset(ones[:, :], 1.0)
            pool.memset(upper[:, :], 1.0).then_inc(iotas, 1)
            pool.wait_ge(iotas, 1)
            pool.affine_select(out=upper[:, :], in_=upper[:, :], compare_op=ALU.is_gt, fill=0.0, base=0,
                               pattern=[[1, P]], channel_multiplier=-1).then_inc(tri, 1)

        @block.scalar
        def _(act):
            act.wait_ge(var_ready, 1)
            act.activation(std[:, :], mv[:, :, 1], ACT.Sqrt, bias=eps[:, :]).then_inc(std_ready, 1)
            with act.Fori(0, NT // 2) as i:
                for p in range(2):
                    t = i * 2 + p
                    act.wait_ge(xt_full, t + 3)
                    act.copy(xnT[p][:, :, :], xt_ps[p][:, :].rearrange("p (c t) -> p c t", c=C)).then_inc(xt_empty, 1)
            act.wait_ge(d4_ready, 1)
            act.activation(e4[:, :, :], d4[:, :, :], ACT.Exp).then_inc(e4_ready, 1)

        @block.tensor
        def _(pe):
            pe.sem_inc(xt_full, 2)
            pe.wait_ge(gw_loaded, DMA)
            with pe.Fori(0, NT // 2) as i:
                for p in range(2):
                    t = i * 2 + p
                    pe.wait_ge(xn_ready, t + 1)
                    for c in range(C):
                        m = pe.transpose(xt_ps[p][:, c * P:(c + 1) * P], xn[p][:, c * P:(c + 1) * P], ident[:, :])
                    m.then_inc(xt_full, 1)
                    pe.wait_ge(xt_empty, t + 1)
                    pe.wait_ge(lg_empty, t + 1)
                    for c in range(C):
                        m = pe.matmul(lg_ps[p][:, 0:E_], xnT[p][:, c, :], gw[:, c, :], start=(c == 0),
                                      stop=(c == C - 1))
                    m.then_inc(lg_full, 1)
            pe.wait_ge(tri, 1)
            pe.wait_ge(mask_ready, 1)
            pe.matmul(pos_ps[:, :, :], upper[:, :], mask[:, :, :], start=True, stop=True)
            for t in range(NT - 1):
                m = pe.matmul(pos_ps[:, t + 1:NT, :], ones[:, :],
                              mask[:, t:t + 1, :].broadcast_to([P, NT - 1 - t, E_]),
                              start=False, stop=True, skip_group_check=True)
            for t in range(NT):
                m = pe.matmul(cnt_ps[:, 0:E_], ones[:, :], mask[:, t, :], start=(t == 0), stop=(t == NT - 1))
            m.then_inc(pos_full, 1)
            with pe.Fori(0, NT) as t:
                for k in range(K_):
                    pe.wait_ge(tabs_in, t * K_ + k + 1)
                    pe.matmul(tab_ps[:, 0:2 * NS], ohr[k][:, :], ohq[k][:, :, :].rearrange("p a n -> p (a n)"),
                              start=False, stop=True, skip_group_check=True).then_inc(tab_used, 1)

        @block.vector
        def _(dve):
            made = [0]

            def done(ins):
                made[0] += 1
                ins.then_inc(step, 1)
                dve.wait_ge(step, made[0])

            dve.sem_inc(lg_empty, 2)
            dve.sem_inc(tab_used, K_)
            dve.memset(eps[:, :], EPS)
            for t in range(NT):
                s = dve.bn_stats(st6[:, t, :], xs[:, t, :])
            done(s)
            for t in range(NT):
                s = dve.bn_aggr(mv[:, t, :], st6[:, t, :])
            s.then_inc(var_ready, 1)
            dve.wait_ge(std_ready, 1)
            done(dve.reciprocal(rstd[:, :], std[:, :]))

            def normalise(t, p):
                dve.wait_ge(xt_full, t + 1)
                dve.wait_ge(xn_stored[p], (t - p) * (DMA // 2) + DMA)
                dve.tensor_scalar(xn[p][:, :], xs[:, bass.ds(t, 1), :].rearrange("p a d -> p (a d)"),
                                  mv[:, bass.ds(t, 1), 0], rstd[:, bass.ds(t, 1)], ALU.subtract,
                                  ALU.mult).then_inc(xn_ready, 1)

            def logits(t, p):
                dve.wait_ge(lg_full, t + 1)
                dve.tensor_copy(lg[:, bass.ds(t, 1), :].rearrange("p a e -> p (a e)"),
                                lg_ps[p][:, 0:E_]).then_inc(lg_empty, 1)

            normalise(0, 0)
            with dve.Fori(0, NT // 2 - 1) as i:
                for p in range(2):
                    normalise(i * 2 + p + 1, (p + 1) % 2)
                    logits(i * 2 + p, p)
            normalise(NT - 1, 1)
            logits(NT - 2, 0)
            logits(NT - 1, 1)
            dve.wait_ge(lg_empty, NT + 2)
            for t in range(NT):
                s = dve.max(top[:, t, :], lg[:, t, :])
            done(s)
            for t in range(NT):
                s = dve.max_index(idx[:, t, :], top[:, t, :], lg[:, t, :])
            done(s)
            dve.tensor_tensor(d4[:, :, :], top[:, :, 0:K_], top[:, :, 0:1].broadcast_to([P, NT, K_]),
                              ALU.subtract).then_inc(d4_ready, 1)
            done(dve.tensor_copy(idf[:, :, :], idx[:, :, 0:K_]))
            dve.wait_ge(iotas, 1)
            ie = iota_e[:, :].unsqueeze(1).broadcast_to([P, NT, E_])
            for k in range(K_):
                s = dve.tensor_tensor(oh[:, :, k, :], ie, idf[:, :, k:k + 1].broadcast_to([P, NT, E_]), ALU.is_equal)
            done(s)
            dve.tensor_tensor(m1[:, :, :], oh[:, :, 0, :], oh[:, :, 1, :], ALU.add)
            done(dve.tensor_tensor(m2[:, :, :], oh[:, :, 2, :], oh[:, :, 3, :], ALU.add))
            dve.tensor_tensor(mask[:, :, :], m1[:, :, :], m2[:, :, :], ALU.add).then_inc(mask_ready, 1)
            dve.wait_ge(e4_ready, 1)
            done(dve.tensor_reduce(s4[:, :, :], e4[:, :, :], AX.X, ALU.add))
            done(dve.reciprocal(r4[:, :, :], s4[:, :, :]))
            dve.tensor_tensor(w4[:, :, :], e4[:, :, :], r4[:, :, :].broadcast_to([P, NT, K_]), ALU.mult)
            dve.wait_ge(pos_full, 1)
            done(dve.tensor_copy(n_e[:, :], cnt_ps[:, 0:E_]))
            done(dve.tensor_tensor(cmp_n[:, :, :], n_e[:, :].unsqueeze(2).broadcast_to([P, E_, NT - 1]),
                                   iota_j[:, :].unsqueeze(1).broadcast_to([P, E_, NT - 1]), ALU.is_gt))
            done(dve.tensor_reduce(sl[:, :], cmp_n[:, :, :], AX.X, ALU.add))
            done(dve.tensor_scalar(sl[:, :], sl[:, :], 1.0, None, ALU.add))
            done(dve.tensor_tensor_scan(cum[:, :], sl[:, :], zero[:, :], 0.0, ALU.add, ALU.add))
            done(dve.tensor_tensor(base[:, :], cum[:, :], sl[:, :], ALU.subtract))
            done(dve.tensor_scalar(base[:, :], base[:, :], float(TILE), None, ALU.mult))
            dve.tensor_copy(cum_i[:, :], cum[:, :])
            done(dve.tensor_tensor(pos[:, :, :], pos_ps[:, :, :], base[:, :].unsqueeze(1).broadcast_to([P, NT, E_]),
                                   ALU.add))
            for k in range(K_):
                s = dve.tensor_tensor(pr[:, :, k, :], oh[:, :, k, :], pos[:, :, :], ALU.mult)
            done(s)
            done(dve.tensor_reduce(destf[:, :, :], pr[:, :, :, :], AX.X, ALU.add))
            dve.tensor_copy(dest[:, :, :], destf[:, :, :])
            done(dve.tensor_copy(desti[:, :, :], destf[:, :, :]))
            dve.tensor_scalar(qi[:, :, :], desti[:, :, :], 7, None, ALU.arith_shift_right)
            done(dve.tensor_scalar(ri[:, :, :], desti[:, :, :], P - 1, None, ALU.bitwise_and))
            dve.tensor_copy(qf[:, :], qi[:, :, :].rearrange("p t k -> p (t k)"))
            dve.tensor_copy(rf[:, :], ri[:, :, :].rearrange("p t k -> p (t k)"))
            done(dve.tensor_tensor(cmp_s[:, :, :], iota_s[:, :].unsqueeze(2).broadcast_to([P, NS, E_]),
                                   cum[:, :].unsqueeze(1).broadcast_to([P, NS, E_]), ALU.is_ge))
            done(dve.tensor_reduce(sef[:, :], cmp_s[:, :, :], AX.X, ALU.add))
            done(dve.tensor_scalar(sef[:, :], sef[:, :], float(E_ - 1), None, ALU.min))
            done(dve.tensor_copy(slot_e[:, :], sef[:, :]))
            dve.tensor_scalar(slot_buf[:, :], slot_e[:, :], NW - 1, None, ALU.bitwise_and)
            done(dve.memset(tab_ps[:, 0:2 * NS], 0.0))
            with dve.Fori(0, NT) as t:
                for k in range(K_):
                    dve.wait_ge(tab_used, t * K_ + k + 1)
                    q1, r1 = qf[:, bass.ds(t * K_ + k, 1)], rf[:, bass.ds(t * K_ + k, 1)]
                    dve.tensor_scalar(ohr[k][:, :], iota_r[:, :], r1, None, ALU.is_equal)
                    dve.tensor_scalar(ohq[k][:, 0, :], iota_q[:, :], q1, row[:, :], ALU.is_equal, ALU.mult)
                    dve.tensor_scalar(ohq[k][:, 1, :], iota_q[:, :], q1, tcol[:, bass.ds(t, 1)], ALU.is_equal,
                                      ALU.mult).then_inc(tabs_in, 1)
            dve.wait_ge(tab_used, NT * K_ + K_)
            done(dve.tensor_copy(tabf[:, :], tab_ps[:, 0:NS]))
            done(dve.scalar_tensor_tensor(tabf[:, :], tab_ps[:, NS:2 * NS], float(P), tabf[:, :], ALU.mult, ALU.add))
            done(dve.tensor_copy(tok[:, :], tabf[:, :]))


def experts(nc, wgu_l, wgu_s, wd_l, wd_s, xs, ident, xd, yd, tabs, out):
    w4, dest, tok, slot_e, slot_buf, cum_i = tabs
    with ExitStack() as ctx:
        sb = lambda n, s, d: ctx.enter_context(nc.sbuf_tensor(n, s, d))
        ps = lambda n, s: ctx.enter_context(nc.psum_tensor(n, s, F32))
        sem = lambda n: ctx.enter_context(nc.semaphore(n))

        GU = sb("GU", [P, NW, C, 2, IW], F32)
        DW = sb("DW", [P, NW, 3, D], F32)
        idx = [sb(f"gidx{i}", [P, 1], U32) for i in range(2)]
        xg = [sb(f"xg{i}", [P, D], F32) for i in range(2)]
        xT = [sb(f"xT{i}", [P, C, P], F32) for i in range(2)]
        sg = [sb(f"sg{i}", [P, IW], F32) for i in range(2)]
        a = [sb(f"a{i}", [P, IW], F32) for i in range(2)]
        aT = [sb(f"aT{i}", [P, 3, P], F32) for i in range(2)]
        yb = [sb(f"yb{i}", [P, D], F32) for i in range(2)]
        yidx = [sb(f"yidx{i}", [P, K_], U32) for i in range(2)]
        yg = [sb(f"yg{i}", [P, K_, D], F32) for i in range(2)]

        xt_ps = [ps(f"xt_ps{i}", [P, 512]) for i in range(2)]
        g_ps = [ps(f"g_ps{i}", [P, 512]) for i in range(2)]
        u_ps = [ps(f"u_ps{i}", [P, 512]) for i in range(2)]
        at_ps, y_ps = ps("at_ps", [P, 4, P]), ps("y_ps", [P, D])

        w_loaded = [sem(f"w_loaded{i}") for i in range(NW)]
        experts_ready, slots_done = sem("experts_ready"), sem("slots_done")
        idx_ready, x_loaded = sem("idx_ready"), [sem(f"xg_loaded{i}") for i in range(2)]
        xt_full, xt_empty, gu_full = sem("xt_full2"), sem("xt_empty2"), sem("gu_full")
        sg_ready, a_ready, at_full, at_empty = sem("sg_ready"), sem("a_ready"), sem("at_full"), sem("at_empty")
        y_empty, y_stored = sem("y_empty"), [sem(f"y_stored{i}") for i in range(2)]
        yi_ready, yg_loaded = sem("yi_ready"), [sem(f"yg_loaded{i}") for i in range(2)]
        passed = sem("e_passed")
        yg_used, added, out_stored = sem("yg_used"), sem("added"), sem("out_stored")

        block = ctx.enter_context(nc.Block())

        @block.sync
        def _(sp):
            def load(i, p):
                e = i * 2 + p
                gl = wgu_l[bass.ds(e, 1)].rearrange("e p n f -> (e p) n f")
                gs = wgu_s[bass.ds(i, 1)].rearrange("e p n f -> (e p) n f")
                dst = GU[:, p].rearrange("p c g f -> p (c g) f")
                sp.dma_start(dst[:, :, 0:IL], gl).then_inc(w_loaded[p], DMA)
                sp.dma_start(dst[:, :, IL:IW], gs).then_inc(w_loaded[p], DMA)
                dl = wd_l[bass.ds(e, 1)].rearrange("e r d -> (e r) d")
                ds = wd_s[bass.ds(i, 1)].rearrange("e r d -> (e r) d")
                sp.dma_start(DW[:, p, 0, :], dl[0:P, :]).then_inc(w_loaded[p], DMA)
                sp.dma_start(DW[0:IL - P, p, 1, :], dl[P:IL, :]).then_inc(w_loaded[p], DMA)
                sp.dma_start(DW[:, p, 2, :], ds).then_inc(w_loaded[p], DMA)

            def arrived(i, p):
                sp.wait_ge(w_loaded[p], i * 5 * DMA + 5 * DMA)
                sp.sem_inc(experts_ready, 1)

            load(0, 0)
            load(0, 1)
            arrived(0, 0)
            arrived(0, 1)
            with sp.Fori(1, E_ // 2) as i:
                for p in range(2):
                    last = sp.value_load(cum_i[0:1, bass.ds(i * 2 + p - 2, 1)], min_val=1, max_val=NS)
                    sp.wait_ge(slots_done, last)
                    load(i, p)
                    arrived(i, p)
            with sp.Fori(0, NT) as t:
                sp.wait_ge(added, t * K_ + K_)
                sp.dma_start(out[bass.ds(t * P, P), :],
                             xs[:, bass.ds(t, 1), :].rearrange("p a d -> p (a d)")).then_inc(out_stored, DMA)
            sp.wait_ge(out_stored, NT * DMA)

        @block.gpsimd
        def _(pool):
            with pool.Fori(0, NS // 2) as i:
                for p in range(2):
                    s = i * 2 + p
                    pool.wait_ge(xt_full, s + 1)
                    pool.tensor_copy(idx[p][:, :], tok[:, bass.ds(s, 1)]).then_inc(idx_ready, 1)
                    pool.wait_ge(idx_ready, s + 1)
                    pool.sem_inc(passed, 1)
                    pool.indirect_dma_start(xg[p][:, :], None, xd[:, :], bass.IndirectOffsetOnAxis(idx[p][:, :], 0))\
                        .then_inc(x_loaded[p], DMA)
            for p in range(2):
                pool.wait_ge(y_stored[p], DMA * (NS // 2 + 1))
            with pool.Fori(0, NT // 2) as i:
                for p in range(2):
                    t = i * 2 + p
                    pool.wait_ge(yg_used, t + 1)
                    pool.tensor_copy(yidx[p][:, :], dest[:, bass.ds(t, 1), :].rearrange("p a k -> p (a k)"))\
                        .then_inc(yi_ready, 1)
                    pool.wait_ge(yi_ready, t + 1)
                    pool.sem_inc(passed, 1)
                    for k in range(K_):
                        pool.indirect_dma_start(yg[p][:, k, :], None, yd[:, :],
                                                bass.IndirectOffsetOnAxis(yidx[p][:, k:k + 1], 0))\
                            .then_inc(yg_loaded[p], DMA)

        def slots(eng, first, body, last):
            first()
            with eng.Fori(1, NS // 2 - 1) as i:
                body(i * 2, 0)
                body(i * 2 + 1, 1)
            last()

        @block.scalar
        def _(act):
            act.sem_inc(y_stored[0], DMA)
            act.sem_inc(y_stored[1], DMA)

            def x_evac(s, p):
                act.wait_ge(xt_full, s + 3)
                act.copy(xT[p][:, :, :], xt_ps[p][:, :].rearrange("p (c t) -> p c t", c=C)).then_inc(xt_empty, 1)

            def silu(s, p):
                act.wait_ge(gu_full, s + 1)
                act.activation(sg[p][:, :], g_ps[p][:, 0:IW], ACT.Silu).then_inc(sg_ready, 1)

            def y_evac(s, p):
                act.wait_ge(slots_done, s + 1)
                act.wait_ge(y_stored[p], (s - p) * (DMA // 2) + DMA)
                act.copy(yb[p][:, :], y_ps[:, :]).then_inc(y_empty, 1)
                act.wait_ge(y_empty, s + 1)
                act.dma_start(yd[bass.ds(s * TILE, TILE), :], yb[p][:, :]).then_inc(y_stored[p], DMA)

            def slot(s, p, first=False, last=False):
                if not last:
                    x_evac(s + 1, 1 - p)
                silu(s, p)
                if not first:
                    y_evac(s - 1, 1 - p)

            x_evac(0, 0)
            slot(0, 0, first=True)
            slot(1, 1)
            with act.Fori(1, NS // 2 - 1) as i:
                slot(i * 2, 0)
                slot(i * 2 + 1, 1)
            slot(NS - 2, 0)
            slot(NS - 1, 1, last=True)
            y_evac(NS - 1, 1)

        @block.vector
        def _(dve):
            def at_evac(s, p):
                dve.wait_ge(at_full, s + 1)
                dve.tensor_copy(aT[p][:, 0::2, :], at_ps[:, 0:3:2, :])
                dve.tensor_copy(aT[p][0:IL - P, 1, :], at_ps[0:IL - P, 1, :]).then_inc(at_empty, 1)

            def gated(s, p):
                dve.wait_ge(sg_ready, s + 1)
                dve.tensor_tensor(a[p][:, 0:IL], u_ps[p][:, 0:IL], sg[p][:, 0:IL], ALU.mult)
                dve.scalar_tensor_tensor(a[p][:, IL:IW], u_ps[p][:, IL:IW], SMALL, sg[p][:, IL:IW], ALU.mult,
                                         ALU.mult).then_inc(a_ready, 1)

            gated(0, 0)
            at_evac(0, 0)
            gated(1, 1)
            with dve.Fori(1, NS // 2) as i:
                for p in range(2):
                    at_evac(i * 2 + p - 1, 1 - p)
                    gated(i * 2 + p, p)
            at_evac(NS - 1, 1)
            dve.sem_inc(yg_used, 2)
            with dve.Fori(0, NT // 2) as i:
                for p in range(2):
                    t = i * 2 + p
                    dve.wait_ge(yg_loaded[p], i * K_ * DMA + K_ * DMA)
                    xt = xs[:, bass.ds(t, 1), :].rearrange("p a d -> p (a d)")
                    for k in range(K_):
                        w = w4[:, bass.ds(t, 1), k]
                        ins = dve.scalar_tensor_tensor(xt, yg[p][:, k, :], w, xt, ALU.mult, ALU.add)
                        ins.then_inc(added, 1)
                        dve.wait_ge(added, t * K_ + k + 1)
                    dve.sem_inc(yg_used, 1)

        @block.tensor
        def _(pe):
            pe.sem_inc(xt_full, 2)

            def transpose_x(s, p):
                if p is not None:
                    pe.wait_ge(x_loaded[p], (s - p) * (DMA // 2) + DMA)
                for c in range(C):
                    m = pe.transpose(xt_ps[p][:, c * P:(c + 1) * P], xg[p][:, c * P:(c + 1) * P], ident[:, :])
                m.then_inc(xt_full, 1)

            def gate_up(s, p, buf):
                pe.wait_ge(xt_empty, s + 1)
                for ps_, g in ((g_ps, 0), (u_ps, 1)):
                    for c in range(C):
                        m = pe.matmul(ps_[p][:, 0:IW], xT[p][:, c, :],
                                      GU[:, bass.ds(buf, 1), c, g, :].rearrange("p a f -> p (a f)"),
                                      start=(c == 0), stop=(c == C - 1))
                m.then_inc(gu_full, 1)

            def transpose_a(s, p):
                pe.wait_ge(a_ready, s + 1)
                pe.transpose(at_ps[:, 0, :], a[p][:, 0:P], ident[:, :])
                pe.transpose(at_ps[0:IL - P, 1, :], a[p][:, P:IL], ident[:, :])
                pe.transpose(at_ps[:, 2, :], a[p][:, IL:IW], ident[:, :]).then_inc(at_full, 1)

            def down(s, p, buf):
                pe.wait_ge(at_empty, s + 1)
                if not (isinstance(s, int) and s == 0):
                    pe.wait_ge(y_empty, s)
                for c in range(3):
                    rows = slice(0, IL - P) if c == 1 else slice(0, P)
                    m = pe.matmul(y_ps[:, :], aT[p][rows, c, :],
                                  DW[rows, bass.ds(buf, 1), c, :].rearrange("p a d -> p (a d)"),
                                  start=(c == 0), stop=(c == 2))
                m.then_inc(slots_done, 1)

            def slot(s, p, first=False, last=False):
                e = pe.value_load(slot_e[0:1, bass.ds(s, 1)], min_val=0, max_val=E_ - 1)
                buf = pe.value_load(slot_buf[0:1, bass.ds(s, 1)], min_val=0, max_val=NW - 1)
                if not first:
                    transpose_a(s - 1, 1 - p)
                if not last:
                    transpose_x(s + 1, 1 - p)
                pe.wait_ge(experts_ready, e + 1)
                gate_up(s, p, buf)
                if not first:
                    down(s - 1, 1 - p, pe.value_load(slot_buf[0:1, bass.ds(s - 1, 1)], min_val=0, max_val=NW - 1))

            transpose_x(0, 0)
            slot(0, 0, first=True)
            slot(1, 1)
            with pe.Fori(1, NS // 2 - 1) as i:
                slot(i * 2, 0)
                slot(i * 2 + 1, 1)
            slot(NS - 2, 0)
            slot(NS - 1, 1, last=True)
            transpose_a(NS - 1, 1)
            down(NS - 1, 1, pe.value_load(slot_buf[0:1, bass.ds(NS - 1, 1)], min_val=0, max_val=NW - 1))


def build(nc, t, out):
    qd = nc.dram_tensor("qd", (NB, P, 3, C * S), BF16, kind="Internal").ap()
    kd = nc.dram_tensor("kd", (NB, P, 3, S), BF16, kind="Internal").ap()
    md = nc.dram_tensor("md", (NB, 3, H, S), BF16, kind="Internal").ap()
    xd = nc.dram_tensor("xd", (NT * P, D), F32, kind="Internal").ap()
    yd = nc.dram_tensor("yd", (NS * TILE, D), F32, kind="Internal").ap()
    with ExitStack() as ctx:
        sb = lambda n, s, d: ctx.enter_context(nc.sbuf_tensor(n, s, d))
        xs, ident = sb("xs", [P, NT, D], F32), sb("ident", [P, P], F32)
        tabs = (sb("w4", [P, NT, K_], F32), sb("dest", [P, NT, K_], U32), sb("tok", [P, NS], U32),
                sb("slot_e", [P, NS], I32), sb("slot_buf", [P, NS], I32), sb("cum_i", [P, E_], I32))
        attention(nc, t["x"], t["ctx"], t["wq"], t["wk"], t["wv"], t["wfc"], t["bfc"], xs, ident, qd, kd, md)
        route(nc, t["gate_w"], xs, ident, xd, tabs)
        experts(nc, t["wgu_l"], t["wgu_s"], t["wd_l"], t["wd_s"], xs, ident, xd, yd, tabs, out)


def kernel(**inputs):
    import numpy as np
    import concourse.bacc as bacc
    from concourse.bass_utils import run_bass_kernel_spmd

    a = {k: np.asarray(v) for k, v in inputs.items()}
    order = np.arange(D).reshape(G, C, DH).transpose(1, 0, 2).reshape(-1)

    def rows_in(w):
        return w.reshape(C, P, -1).transpose(1, 0, 2)

    def gate_up(g, u):
        n, _, f = g.shape
        return np.stack([g, u], 1).reshape(n, 2, C, P, f).transpose(0, 3, 2, 1, 4).reshape(n, P, 2 * C, f)

    arrays = {
        "x": a["x"].reshape(NT * P, D),
        "ctx": a["ctx_2048"].transpose(0, 2, 1).reshape(NB, C, P, S).transpose(0, 2, 1, 3),
        "wq": rows_in(a["L0_xattn_Wq"].T[:, order]),
        "wk": rows_in(a["L0_xattn_Wk"].T),
        "wv": rows_in(a["L0_xattn_Wv"].T),
        "wfc": rows_in(a["L0_xattn_Wfc"].T),
        "bfc": np.broadcast_to(a["L0_xattn_bfc"], (P, D)),
        "gate_w": rows_in(a["L0_ffn_gate_w"].T),
        "wgu_l": gate_up(a["L0_ffn_Wg"], a["L0_ffn_Wu"]),
        "wgu_s": gate_up(a["L0_ffn_cWg"], a["L0_ffn_cWu"]),
        "wd_l": a["L0_ffn_Wd"],
        "wd_s": a["L0_ffn_cWd"],
    }
    arrays = {f"in_{k}": np.ascontiguousarray(v) for k, v in arrays.items()}
    nc = bacc.Bacc("TRN2", target_bir_lowering=False, num_devices=1)
    t = {k[3:]: nc.dram_tensor(k, v.shape, F32, kind="ExternalInput").ap() for k, v in arrays.items()}
    out = nc.dram_tensor("out_x", (NT * P, D), F32, kind="ExternalOutput").ap()
    build(nc, t, out)
    r = run_bass_kernel_spmd(nc, [arrays], core_ids=[0])
    return r.results[0]["out_x"].reshape(NB, S, D)
```

```python
from contextlib import ExitStack

import concourse.bass as bass
from concourse import mybir

ALU = mybir.AluOpType
ACT = mybir.ActivationFunctionType
AX = mybir.AxisListType
F32 = mybir.dt.float32
I32 = mybir.dt.int32
U32 = mybir.dt.uint32
BF16 = mybir.dt.bfloat16
F16 = mybir.dt.float16

P = 128
D = 512
C = D // P
NB, S = 8, 256
TT = S // P
NT = NB * TT
H, G, DH = 32, 8, 16
J = H // 2
EPS = 1e-5
DMA = 16

RUNS = ((0, 3), (1, 2), (2, 1))
ROWS_QK = DH * sum(n for _, n in RUNS)
ROWS_ST = ROWS_QK + 3
NP = 4
LAG = 3
LEAD = 9
CH = 4
STP = 3
GAIN = 15

KV_AT, XT_AT, OT_AT, FC_AT, QP_AT = (2, 3), (4, 5), (6, 9), ((7, 8), (10, 11)), ((12, 13), (14, 15))


def some(count):
    return not isinstance(count, int) or count > 0


def attention(nc, x_in, ctx_in, wq, wk, wv, wfc, bfc, xs, st_new, ident, qd, kd, md):
    with ExitStack() as ctx:
        sb = lambda n, s, d: ctx.enter_context(nc.sbuf_tensor(n, s, d))
        ps = lambda n, s: ctx.enter_context(nc.psum_tensor(n, s, F32))
        sem = lambda n: ctx.enter_context(nc.semaphore(n))

        Wq, Wfc = sb("Wq", [P, C, D], F32), sb("Wfc", [P, C, D], F32)
        Wk, Wv = sb("Wk", [P, C, P], F32), sb("Wv", [P, C, P], F32)
        Bfc = sb("Bfc", [P, D], F32)
        identb = sb("identb", [P, P], BF16)
        ctxT = sb("ctxT", [P, C, S], F32)
        st6 = sb("st6", [P, NT, 6], F32)
        mv = sb("mv", [P, NT, 2], F32)
        eps, gain = sb("eps", [P, 1], F32), sb("gain", [P, 1], F32)
        std, rstd = sb("std", [P, NT], F32), sb("rstd", [P, NT], F32)
        xn = sb("xn", [P, TT, D], F32)
        xnT = sb("xnT", [P, C, S], F32)
        q3 = sb("q3", [P, 3, C * S], BF16)
        kv = [sb(f"kv{i}", [P, 4, 2 * S], BF16) for i in range(2)]
        qres = [sb(f"qres{i}", [P, 2 * S], F32) for i in range(2)]
        kvres = sb("kvres", [P, 2 * S], F32)
        qst = [sb(f"qst{i}", [P, H, S], BF16) for i in range(2)]
        kst = [sb(f"kst{i}", [P, G, S], BF16) for i in range(2)]
        mx = [sb(f"mx{i}", [P, TT, 2 * CH], F32) for i in range(2)]
        mres = sb("mres", [P, TT, 2 * CH], F32)
        nm = [sb(f"nm{i}", [P, TT, 3, 2 * CH], BF16) for i in range(2)]
        mts = [sb(f"mts{i}", [6 * CH, S], BF16) for i in range(2)]
        pt = [sb(f"pt{i}", [P, 2, TT, S], F32) for i in range(2)]
        ph = [sb(f"ph{i}", [P, 2, TT, S], F16) for i in range(NP)]
        pl = [sb(f"pl{i}", [P, 2, TT, S], F16) for i in range(NP)]
        rec = [sb(f"rec{i}", [P, TT * C, 1], F32) for i in range(2)]
        av = [sb(f"av{i}", [P, TT * C, DH], F32) for i in range(2)]
        o = [sb(f"o{i}", [P, TT, D], F32) for i in range(2)]
        oT = [sb(f"oT{i}", [P, C, P], F32) for i in range(2)]

        s1 = [ps(f"s1{i}", [P, TT, S]) for i in range(2)]
        stp = [ps(f"stp{i}", [P, TT, S]) for i in range(STP)]
        work = [ps(f"work{i}", [P, 512]) for i in range(2)]
        side = ps("side", [P, 512])
        mt_bank = s1[0][:, :, :].rearrange("p t s -> p (t s)").bitcast(BF16)[0:6 * CH, 0:S]
        side_cols = side[:, :].rearrange("p (c t) -> p c t", c=C)

        w_loaded, passed = sem("a_loaded"), sem("passed")
        kvw_loaded, wq_loaded = sem("kvw_loaded"), sem("wq_loaded")
        GROUPS = ((0, 2), (2, 4), (4, 10), (10, 16))
        x_loaded = [sem(f"x_loaded{n}") for n in range(len(GROUPS))]
        c_loaded = sem("c_loaded")
        ident_ready, set_up = sem("ident_ready"), sem("set_up")
        stats, var_ready, std_ready, rstd_ready = sem("stats"), sem("var_ready"), sem("std_ready"), sem("rstd_ready")
        xn_ready, xb_ready = sem("xn_ready"), sem("xb_ready")
        xt_full, qp_full, kv_full, mt_full = sem("xt_full"), sem("qp_full"), sem("kv_full"), sem("mt_full")
        ot_full, fc_full = sem("ot_full"), sem("fc_full")
        xt_empty, qp_empty, kv_empty, mt_empty = sem("xt_empty"), sem("qp_empty"), sem("kv_empty"), sem("mt_empty")
        av_empty, ot_empty, fc_empty = sem("av_empty"), sem("ot_empty"), sem("fc_empty")
        q_hi, q_mid, q_lo = sem("q_hi"), sem("q_mid"), sem("q_lo")
        kv_hi, kv_mid, kv_lo = sem("kv_hi"), sem("kv_mid"), sem("kv_lo")
        q_stored, k_stored, q_stacked, k_stacked = sem("q_stored"), sem("k_stored"), sem("q_stacked"), sem("k_stacked")
        s1_ready, max_done = sem("s1_ready"), sem("max_done")
        nm_step, nm_done = sem("nm_step"), sem("nm_done")
        m_stored, m_ready = sem("m_stored"), [sem(f"m_ready{i}") for i in range(2)]
        st_ready, exp_done, pl_done, av_done = sem("st_ready"), sem("exp_done"), sem("pl_done"), sem("av_done")
        rec_done, sum_done = sem("rec_done"), sem("sum_done")

        def q_parts(n):
            return [q3[:, l, n * 512:(n + 1) * 512] for l in range(3)]

        def units(eng, unit):
            unit(0, 0, 0)
            with eng.Fori(0, 2) as i:
                unit(1, i * 2 + 1, 1)
                unit(2, i * 2 + 2, 0)
            for u in range(5, NB):
                unit(u, u, u % 2)

        def maxima_of(b, j):
            return b + (j + LEAD) // J, (j + LEAD) % J

        def has_maxima(u, j):
            return u < NB - 1 or j + LEAD < J

        block = ctx.enter_context(nc.Block())

        @block.sync
        def _(sp):
            xv = x_in.rearrange("(t p) d -> p t d", p=P)

            def load_x(k):
                t0, t1 = GROUPS[k]
                sp.dma_start(xs[:, t0:t1, :], xv[:, t0:t1, :]).then_inc(x_loaded[k], DMA)

            def load_ctx(b):
                src = ctx_in[bass.ds(b, 1)].rearrange("b p c t -> (b p) c t")
                sp.dma_start(ctxT[:, :, :], src).then_inc(c_loaded, DMA)

            load_x(0)
            load_ctx(0)
            sp.dma_start(Wk[:, :, :], wk).then_inc(kvw_loaded, DMA)
            sp.dma_start(Wv[:, :, :], wv).then_inc(kvw_loaded, DMA)
            sp.dma_start(Wq[:, :, :], wq).then_inc(wq_loaded, DMA)
            for k in range(1, len(GROUPS)):
                load_x(k)
            sp.dma_start(Wfc[:, :, :], wfc).then_inc(w_loaded, DMA)
            sp.dma_start(Bfc[:, :], bfc).then_inc(w_loaded, DMA)

            def store_q(b):
                sp.wait_ge(q_lo, b * 2 + 2)
                sp.sem_inc(passed, 1)
                dst = qd[bass.ds(b, 1)].rearrange("b l p n -> p (b l) n")
                sp.dma_start(dst, q3[:, :, :]).then_inc(q_stored, DMA)

            def stack_q(b, par):
                sp.wait_ge(q_stored, b * DMA + DMA)
                if not (isinstance(b, int) and b < 2):
                    sp.sem_inc(passed, 1)
                    sp.wait_ge(st_ready, (b - 1) * H)
                src = qd[bass.ds(b, 1)].rearrange("b l (d g) n -> (b l d) (g n)", g=G)
                at = 0
                for l, n in RUNS:
                    dst = qst[par][at:at + n * DH, :, :].rearrange("p h t -> p (h t)")
                    sp.dma_start(dst, src[0:n * DH, :]).then_inc(q_stacked, DMA)
                    at += n * DH

            def stack_k(b, par):
                sp.wait_ge(kv_lo, b + 1)
                sp.sem_inc(passed, 1)
                k_b = kd[bass.ds(b, 1)].rearrange("b l p n -> p (b l) n")
                sp.dma_start(k_b, kv[par][:, 0:3, 0:S]).then_inc(k_stored, DMA)
                if not isinstance(b, int) or b < NB - 1:
                    load_ctx(b + 1)
                sp.wait_ge(k_stored, b * DMA + DMA)
                src = kd[bass.ds(b, 1)].rearrange("b l (d g) n -> (b l) d (g n)", g=G)
                at = 0
                for l, n in RUNS:
                    for _ in range(n):
                        dst = kst[par][at:at + DH, :, :].rearrange("p g t -> p (g t)")
                        sp.dma_start(dst, src[l]).then_inc(k_stacked, DMA)
                        at += DH

            def stack_max(b, c, par):
                sp.wait_ge(mt_empty, b * (J // CH) + c + 1)
                m_b = md[bass.ds(b, 1), c].rearrange("b l h s -> (b l h) s")
                sp.dma_start(m_b, mts[c % 2][:, :]).then_inc(m_stored, DMA)
                sp.wait_ge(m_stored, (b * (J // CH) + c) * DMA + DMA)
                heads = slice(c * 2 * CH, (c + 1) * 2 * CH)
                sp.dma_start(qst[par][ROWS_QK:ROWS_ST, heads, :], md[bass.ds(b, 1), c].rearrange("b l h s -> (b l) h s"))\
                  .then_inc(m_ready[c % 2], DMA)

            sp.wait_ge(set_up, 1)
            stack_k(0, 0)
            store_q(0)
            stack_q(0, 0)
            store_q(1)
            for j in range(CH, LEAD, CH):
                stack_max(0, j // CH - 1, 0)

            def unit(u, b, par):
                if u < NB - 1:
                    stack_q(b + 1, 1 - par)
                for j in range(J):
                    if (j + LEAD) % CH == 0 and has_maxima(u, j - 1):
                        b1, j1 = maxima_of(b, j - 1)
                        stack_max(b1, j1 // CH, par if j - 1 + LEAD < J else 1 - par)
                    if j == KV_AT[1] + 1 and u < NB - 1:
                        stack_k(b + 1, 1 - par)
                if u < NB - 2:
                    store_q(b + 2)

            units(sp, unit)

        @block.gpsimd
        def _(pool):
            pool.memset(ident[:, :], 0.0).then_inc(ident_ready, 1)
            pool.memset(identb[:, :], 0.0).then_inc(ident_ready, 1)
            pool.wait_ge(ident_ready, 2)
            for eye in (ident, identb):
                pool.affine_select(out=eye[:, :], in_=eye[:, :], compare_op=ALU.not_equal, fill=1.0, base=0,
                                   pattern=[[-1, P]], channel_multiplier=1).then_inc(ident_ready, 1)
            for i in range(2):
                pool.memset(kst[i][:, :, :], 1.0)
                m = pool.memset(kv[i][:, 3, :], 1.0)
            m.then_inc(set_up, 1)

            def add_bias(b):
                for t in range(TT):
                    tile = b * TT + t
                    pool.wait_ge(xn_ready, tile + 1)
                    xt = xs[:, bass.ds(tile, 1), :].rearrange("p a d -> p (a d)")
                    pool.tensor_tensor(xt, xt, Bfc[:, :], ALU.add).then_inc(xb_ready, 1)

            def third_part(b, n):
                pool.wait_ge(q_mid, b * 2 + n + 1)
                pool.tensor_tensor(q_parts(n)[2], qres[n][:, :], q_parts(n)[1], ALU.subtract).then_inc(q_lo, 1)

            for b in range(2):
                for n in range(2):
                    third_part(b, n)
                if b == 0:
                    pool.wait_ge(w_loaded, 2 * DMA)
                add_bias(b)

            def unit(u, b, par):
                for j in range(J):
                    pool.wait_ge(exp_done, b * H + 2 * j + 2)
                    pool.tensor_tensor(pl[j % NP][:, :, :, :], pt[j % 2][:, :, :, :], ph[j % NP][:, :, :, :],
                                       ALU.subtract).then_inc(pl_done, 1)
                    if u < NB - 2:
                        if j == XT_AT[0]:
                            add_bias(b + 2)
                        for n in range(2):
                            if j == QP_AT[n][1]:
                                third_part(b + 2, n)

            units(pool, unit)

        @block.scalar
        def _(act):
            def deviations(k):
                t0, t1 = GROUPS[k]
                act.wait_ge(var_ready, k + 1)
                act.activation(std[:, t0:t1], mv[:, t0:t1, 1], ACT.Sqrt, bias=eps[:, :]).then_inc(std_ready, 1)

            def x_evac(b, t):
                act.wait_ge(xt_full, b * TT + t + 1)
                act.copy(xnT[:, :, t * P:(t + 1) * P], side_cols).then_inc(xt_empty, 1)

            def kv_first(b, par):
                act.wait_ge(kv_full, b + 1)
                act.copy(kv[par][:, 0, :], side[:, :]).then_inc(kv_hi, 1)

            def q_first(b, n):
                if n == 0 and some(b):
                    act.wait_ge(q_stored, b * DMA)
                act.wait_ge(qp_full, b * 2 + n + 1)
                act.copy(q_parts(n)[0], side[:, :]).then_inc(q_hi, 1)

            def o_evac(b, t):
                act.wait_ge(ot_full, b * TT + t + 1)
                act.copy(oT[t][:, :, :], side_cols).then_inc(ot_empty, 1)

            deviations(0)
            kv_first(0, 0)
            deviations(1)
            for b in range(2):
                x_evac(b, 0)
                x_evac(b, 1)
                if b:
                    deviations(2)
                    deviations(3)
                q_first(b, 0)
                q_first(b, 1)

            def unit(u, b, par):
                for j in range(J):
                    n = b * J + j
                    for r in range(2):
                        bank = stp[(2 * j + r) % STP]
                        act.wait_ge(st_ready, b * H + 2 * j + r + 1)
                        if r == 0 and some(n - 1):
                            act.wait_ge(pl_done, n - 1)
                        if r == 0 and some(n + 1 - NP):
                            act.wait_ge(av_done, n + 1 - NP)
                        act.activation(ph[j % NP][:, r, :, :], bank[:, :, :], ACT.Exp, bias=gain[:, :],
                                       scale=DH ** -0.5)
                        act.activation(pt[j % 2][:, r, :, :], bank[:, :, :], ACT.Exp, bias=gain[:, :],
                                       scale=DH ** -0.5).then_inc(exp_done, 1)
                        evacuate(u, b, j, par, r)

            def evacuate(u, b, j, par, r):
                if r == 0 and u < NB - 2 and j in XT_AT:
                    x_evac(b + 2, XT_AT.index(j))
                if r == 0 and u > 0 and j in OT_AT:
                    o_evac(b - 1, OT_AT.index(j))
                if r == 0 and u < NB - 1 and j == KV_AT[1]:
                    kv_first(b + 1, 1 - par)
                for n in range(2):
                    if r == 0 and u < NB - 2 and j == QP_AT[n][1]:
                        q_first(b + 2, n)

            units(act, unit)
            o_evac(NB - 1, 0)
            o_evac(NB - 1, 1)

        @block.vector
        def _(dve):
            dve.memset(eps[:, :], EPS)
            dve.memset(gain[:, :], GAIN * 0.6931471805599453)

            def moments(k):
                dve.wait_ge(x_loaded[k], DMA)
                for t in range(*GROUPS[k]):
                    dve.bn_stats(st6[:, t, :], xs[:, t, :]).then_inc(stats, 1)
                for t in range(*GROUPS[k]):
                    dve.wait_ge(stats, t + 1)
                    m = dve.bn_aggr(mv[:, t, :], st6[:, t, :])
                m.then_inc(var_ready, 1)

            def invert(k):
                t0, t1 = GROUPS[k]
                dve.wait_ge(std_ready, k + 1)
                dve.reciprocal(rstd[:, t0:t1], std[:, t0:t1]).then_inc(rstd_ready, 1)
                dve.wait_ge(rstd_ready, k + 1)

            def normalise(b):
                for t in range(TT):
                    tile = b * TT + t
                    if some(tile - 1):
                        dve.wait_ge(xt_full, tile - 1)
                    dve.tensor_scalar(xn[:, t, :], xs[:, bass.ds(tile, 1), :].rearrange("p a d -> p (a d)"),
                                      mv[:, bass.ds(tile, 1), 0], rstd[:, bass.ds(tile, 1)],
                                      ALU.subtract, ALU.mult).then_inc(xn_ready, 1)

            def kv_residue(b, par):
                dve.wait_ge(kv_hi, b + 1)
                dve.tensor_tensor(kvres[:, :], side[:, :], kv[par][:, 0, :], ALU.subtract).then_inc(kv_empty, 1)

            def kv_second(b, par):
                dve.wait_ge(kv_empty, b + 1)
                dve.tensor_copy(kv[par][:, 1, :], kvres[:, :]).then_inc(kv_mid, 1)

            def kv_third(b, par):
                dve.wait_ge(kv_mid, b + 1)
                dve.tensor_tensor(kv[par][:, 2, :], kvres[:, :], kv[par][:, 1, :], ALU.subtract).then_inc(kv_lo, 1)

            def q_residue(b, n):
                dve.wait_ge(q_hi, b * 2 + n + 1)
                if some(b * 2 + n - 1):
                    dve.wait_ge(q_lo, b * 2 + n - 1)
                dve.tensor_tensor(qres[n][:, :], side[:, :], q_parts(n)[0], ALU.subtract).then_inc(qp_empty, 1)

            def q_second(b, n):
                dve.wait_ge(qp_empty, b * 2 + n + 1)
                dve.tensor_copy(q_parts(n)[1], qres[n][:, :]).then_inc(q_mid, 1)

            def row_max(b, j):
                for r in range(2):
                    h = 2 * (j % CH) + r
                    dve.wait_ge(s1_ready, b * H + 2 * j + r + 1)
                    dve.tensor_reduce(mx[j // CH % 2][:, :, h:h + 1], s1[r][:, :, :], AX.X, ALU.max)\
                       .then_inc(max_done, 1)

            def split_max(b, c):
                m, n = mx[c % 2], nm[c % 2]
                chunk = b * (J // CH) + c
                dve.wait_ge(max_done, (chunk + 1) * 2 * CH)
                dve.tensor_scalar(n[:, :, 0, :], m[:, :, :], -1.0, None, ALU.mult).then_inc(nm_step, 1)
                dve.wait_ge(nm_step, chunk * 3 + 1)
                dve.scalar_tensor_tensor(mres[:, :, :], m[:, :, :], -1.0, n[:, :, 0, :], ALU.mult,
                                         ALU.subtract).then_inc(nm_step, 1)
                dve.wait_ge(nm_step, chunk * 3 + 2)
                dve.tensor_copy(n[:, :, 1, :], mres[:, :, :]).then_inc(nm_step, 1)
                dve.wait_ge(nm_step, chunk * 3 + 3)
                dve.tensor_tensor(n[:, :, 2, :], mres[:, :, :], n[:, :, 1, :], ALU.subtract).then_inc(nm_done, 1)

            def max_evac(b, c):
                chunk = b * (J // CH) + c
                if some(chunk - 1):
                    dve.wait_ge(m_stored, (chunk - 1) * DMA)
                dve.wait_ge(mt_full, chunk + 1)
                dve.tensor_copy(mts[c % 2][:, :], mt_bank).then_inc(mt_empty, 1)

            def weigh(b, g, par):
                dve.wait_ge(av_done, b * J + 2 * g + 2)
                v = work[g % 2][:, :].rearrange("p (h l d) -> p h l d", l=4, d=DH)
                dve.reciprocal(rec[g % 2][:, :, :], v[:, :, 3, 0:1]).then_inc(rec_done, 1)
                dve.tensor_reduce(av[g % 2][:, :, :].unsqueeze(3), v[:, :, 0:3, :].rearrange("p h l d -> p h d l"),
                                  AX.X, ALU.add).then_inc(sum_done, 1)
                dve.wait_ge(rec_done, b * G + g + 1)
                dve.wait_ge(sum_done, b * G + g + 1)
                dst = o[par][:, :, g * 64:(g + 1) * 64].rearrange("p t (h d) -> p t h d", h=C)
                dve.tensor_tensor(dst, av[g % 2][:, :, :].rearrange("p (t h) d -> p t h d", t=TT),
                                  rec[g % 2][:, :, :].rearrange("p (t h) d -> p t h d", t=TT)
                                  .broadcast_to([P, TT, C, DH]), ALU.mult).then_inc(av_empty, 1)

            def add_out(b, t):
                tile = b * TT + t
                dve.wait_ge(xb_ready, tile + 1)
                dve.wait_ge(fc_full, tile + 1)
                xt = xs[:, bass.ds(tile, 1), :].rearrange("p a d -> p (a d)")
                dve.tensor_tensor(xt, side[:, :], xt, ALU.add).then_inc(fc_empty, 1)
                dve.wait_ge(fc_empty, tile + 1)
                dve.sem_inc(passed, 1)
                dve.bn_stats(st_new[:, bass.ds(tile, 1), :].rearrange("p a d -> p (a d)"), xt)

            moments(0)
            invert(0)
            normalise(0)
            kv_residue(0, 0)
            kv_second(0, 0)
            kv_third(0, 0)
            moments(1)
            invert(1)
            q_residue(0, 0)
            q_second(0, 0)
            moments(2)
            q_residue(0, 1)
            q_second(0, 1)
            normalise(1)
            moments(3)
            invert(2)
            invert(3)
            q_residue(1, 0)
            q_second(1, 0)
            q_residue(1, 1)
            q_second(1, 1)
            for j in range(LEAD):
                if j and j % CH == 0:
                    max_evac(0, j // CH - 1)
                row_max(0, j)
                if j % CH == CH - 1:
                    split_max(0, j // CH)

            def unit(u, b, par):
                for j in range(J):
                    b1, j1 = maxima_of(b, j)
                    if j1 % CH == 0 and has_maxima(u, j - 1):
                        b0, j0 = maxima_of(b, j - 1)
                        max_evac(b0, j0 // CH)
                    if j == XT_AT[0] - 2 and u < NB - 2:
                        normalise(b + 2)
                    for t in range(TT):
                        if u > 0 and j == FC_AT[t][1]:
                            add_out(b - 1, t)
                    if has_maxima(u, j):
                        row_max(b1, j1)
                    for t in range(TT):
                        if u < NB - 2 and j == QP_AT[t][1]:
                            q_residue(b + 2, t)
                            q_second(b + 2, t)
                    if u < NB - 1 and j == KV_AT[1]:
                        kv_residue(b + 1, 1 - par)
                        kv_second(b + 1, 1 - par)
                    if u < NB - 1 and j == KV_AT[1]:
                        kv_third(b + 1, 1 - par)
                    if has_maxima(u, j):
                        if j1 % CH == CH - 1:
                            split_max(b1, j1 // CH)
                    if j % 2 and j >= 5:
                        weigh(b, (j - 5) // 2, par)
                    elif j % 2 and u > 0:
                        weigh(b - 1, (j + 11) // 2, 1 - par)

            units(dve, unit)
            last = (NB - 1) % 2
            weigh(NB - 1, 6, last)
            weigh(NB - 1, 7, last)
            add_out(NB - 1, 0)
            add_out(NB - 1, 1)

        @block.tensor
        def _(pe):
            def transpose_x(b, t):
                pe.wait_ge(xn_ready, b * TT + t + 1)
                if t:
                    pe.wait_ge(xt_empty, b * TT + 1)
                elif isinstance(b, int) and b == 1:
                    pe.wait_ge(qp_empty, 2)
                elif isinstance(b, int) and b == 0:
                    pe.wait_ge(kv_empty, 1)
                else:
                    pe.wait_ge(kv_empty, b)
                for c in range(C):
                    m = pe.transpose(side[:, c * P:(c + 1) * P], xn[:, t, c * P:(c + 1) * P], ident[:, :])
                m.then_inc(xt_full, 1)

            def project_q(b, n, k):
                for c in range(C):
                    m = pe.matmul(side[:, k * S:(k + 1) * S], Wq[:, c, (2 * n + k) * P:(2 * n + k + 1) * P],
                                  xnT[:, c, :], start=(c == 0), stop=(c == C - 1))
                if k:
                    m.then_inc(qp_full, 1)

            def project_k(b):
                pe.wait_ge(c_loaded, b * DMA + DMA)
                for c in range(C):
                    pe.matmul(side[:, 0:S], Wk[:, c, :], ctxT[:, c, :], start=(c == 0), stop=(c == C - 1))

            def project_v(b):
                for t in range(TT):
                    for c in range(C):
                        m = pe.matmul(side[:, S + t * P:S + (t + 1) * P], ctxT[:, c, t * P:(t + 1) * P],
                                      Wv[:, c, :], start=(c == 0), stop=(c == C - 1))
                m.then_inc(kv_full, 1)

            def scores_for_max(b, j, par):
                if j == 0:
                    pe.wait_ge(k_stacked, b * 6 * DMA + 6 * DMA)
                    pe.wait_ge(q_stacked, b * 3 * DMA + 3 * DMA)
                if j % CH == 0 and some(b * (J // CH) + j // CH):
                    pe.wait_ge(mt_empty, b * (J // CH) + j // CH)
                for r in range(2):
                    if some(b * H + 2 * j + r - 1):
                        pe.wait_ge(max_done, b * H + 2 * j + r - 1)
                    for t in range(TT):
                        m = pe.matmul(s1[r][:, t, :], qst[par][0:ROWS_QK, 2 * j + r, t * P:(t + 1) * P],
                                      kst[par][0:ROWS_QK, j // 2, :], start=True, stop=True)
                    m.then_inc(s1_ready, 1)

            def scores(b, j, par):
                if j % CH == 0:
                    c = j // CH
                    pe.wait_ge(m_ready[c % 2], (b * (J // CH // 2) + c // 2) * DMA + DMA)
                for r in range(2):
                    h = 2 * j + r
                    last = h - STP if h >= STP else max(n for n in range(H) if n % STP == h) - H
                    if some(b * H + last + 1):
                        pe.wait_ge(exp_done, b * H + last + 1)
                    for t in range(TT):
                        m = pe.matmul(stp[h % STP][:, t, :], kst[par][0:ROWS_ST, j // 2, t * P:(t + 1) * P],
                                      qst[par][0:ROWS_ST, h, :], start=True, stop=True)
                    m.then_inc(st_ready, 1)

            def values(b, j, par):
                g = j // 2
                if j % 2 == 0 and some(b * G + g - 1):
                    pe.wait_ge(av_empty, b * G + g - 1)
                w = work[g % 2][:, :].rearrange("p (t h l d) -> p t h l d", t=TT, h=C, l=4)
                pe.wait_ge(pl_done, b * J + j + 1)
                for r in range(2):
                    for t in range(TT):
                        for k in range(TT):
                            for part in (ph, pl):
                                m = pe.matmul(w[:, t, 2 * (j % 2) + r], part[j % NP][:, r, k, t * P:(t + 1) * P],
                                              kv[par][:, :, S + k * P + g * DH:S + k * P + (g + 1) * DH],
                                              start=(k == 0 and part is ph), stop=(k == TT - 1 and part is pl))
                m.then_inc(av_done, 1)

            def transpose_max(b, c):
                pe.wait_ge(nm_done, b * (J // CH) + c + 1)
                for t in range(TT):
                    m = pe.transpose(mt_bank[:, t * P:(t + 1) * P], nm[c % 2][:, t].rearrange("p l h -> p (l h)"),
                                     identb[:, :])
                m.then_inc(mt_full, 1)

            def transpose_o(b, t, par):
                if t:
                    pe.wait_ge(fc_empty, b * TT + 1)
                else:
                    pe.wait_ge(av_empty, b * G + G)
                for c in range(C):
                    m = pe.transpose(side[:, c * P:(c + 1) * P], o[par][:, t, c * P:(c + 1) * P], ident[:, :])
                m.then_inc(ot_full, 1)

            def project_out(b, t, half):
                pe.wait_ge(ot_empty, b * TT + t + 1)
                for c in (0, 1) if half == 0 else (2, 3):
                    m = pe.matmul(side[:, :], oT[t][:, c, :], Wfc[:, c, :], start=(c == 0), stop=(c == C - 1))
                if half:
                    m.then_inc(fc_full, 1)

            pe.wait_ge(kvw_loaded, 2 * DMA)
            project_k(0)
            project_v(0)
            pe.wait_ge(ident_ready, 4)
            for b in range(2):
                for t in range(TT):
                    transpose_x(b, t)
                pe.wait_ge(wq_loaded, DMA)
                pe.wait_ge(xt_empty, b * TT + 2)
                for n in range(2):
                    if n:
                        pe.wait_ge(qp_empty, b * 2 + 1)
                    project_q(b, n, 0)
                    project_q(b, n, 1)
            for j in range(LEAD):
                if j and j % CH == 0:
                    transpose_max(0, j // CH - 1)
                scores_for_max(0, j, 0)
            pe.wait_ge(w_loaded, 2 * DMA)

            def side_item(u, b, j, par):
                if u < NB - 2 and j in XT_AT:
                    transpose_x(b + 2, XT_AT.index(j))
                if u < NB - 1 and j == KV_AT[0]:
                    pe.wait_ge(qp_empty, (b + 2) * 2)
                    project_k(b + 1)
                if u < NB - 1 and j == KV_AT[1]:
                    project_v(b + 1)
                if u > 0 and j in OT_AT:
                    if j == OT_AT[0] and u < NB - 2:
                        pe.wait_ge(xt_empty, (b + 3) * TT)
                    elif j == OT_AT[0] and u < NB - 1:
                        pe.wait_ge(kv_empty, b + 2)
                    elif j == OT_AT[0]:
                        pe.wait_ge(fc_empty, (b - 1) * TT)
                    transpose_o(b - 1, OT_AT.index(j), 1 - par)
                for t in range(TT):
                    if u > 0 and j in FC_AT[t]:
                        project_out(b - 1, t, FC_AT[t].index(j))
                    if u < NB - 2 and j in QP_AT[t]:
                        if j == QP_AT[1][0]:
                            pe.wait_ge(qp_empty, (b + 2) * 2 + 1)
                        elif j == QP_AT[0][0] and u > 0:
                            pe.wait_ge(fc_empty, b * TT)
                        elif j == QP_AT[0][0]:
                            pe.wait_ge(xt_empty, (b + 3) * TT)
                        project_q(b + 2, t, QP_AT[t].index(j))

            def unit(u, b, par):
                for j in range(J):
                    scores(b, j, par)
                    side_item(u, b, j, par)
                    b1, j1 = maxima_of(b, j)
                    if j1 % CH == 0 and has_maxima(u, j - 1):
                        b0, j0 = maxima_of(b, j - 1)
                        transpose_max(b0, j0 // CH)
                    if has_maxima(u, j):
                        scores_for_max(b1, j1, par if j + LEAD < J else 1 - par)
                    if j >= LAG:
                        values(b, j - LAG, par)
                    elif u > 0:
                        values(b - 1, J + j - LAG, 1 - par)

            units(pe, unit)
            last = (NB - 1) % 2
            for j in range(J - LAG, J):
                values(NB - 1, j, last)
            pe.wait_ge(fc_empty, (NB - 1) * TT)
            for t in range(TT):
                transpose_o(NB - 1, t, last)
                project_out(NB - 1, t, 0)
                project_out(NB - 1, t, 1)


E_, K_ = 32, 4
TILE = P
NS = (NT * P * K_) // TILE + E_
IL, IS = 192, 128
IW = IL + IS
SMALL = 0.05
NW = 2
NX = 4
XW = D + E_


def load_expert(sp, weights, GU, DW, loaded, i, p):
    wgu_l, wgu_s, wd_l, wd_s = weights
    e = i * 2 + p
    gl = wgu_l[bass.ds(e, 1)].rearrange("e p n f -> (e p) n f")
    gs = wgu_s[bass.ds(i, 1)].rearrange("e p n f -> (e p) n f")
    dst = GU[:, p].rearrange("p c g f -> p (c g) f")
    sp.dma_start(dst[:, :, 0:IL], gl).then_inc(loaded[p], DMA)
    sp.dma_start(dst[:, :, IL:IW], gs).then_inc(loaded[p], DMA)
    dl = wd_l[bass.ds(e, 1)].rearrange("e r d -> (e r) d")
    ds = wd_s[bass.ds(i, 1)].rearrange("e r d -> (e r) d")
    sp.dma_start(DW[:, p, 0, :], dl[0:P, :]).then_inc(loaded[p], DMA)
    sp.dma_start(DW[0:IL - P, p, 1, :], dl[P:IL, :]).then_inc(loaded[p], DMA)
    sp.dma_start(DW[:, p, 2, :], ds).then_inc(loaded[p], DMA)


def route(nc, gate_w, xs, st6, ident, xd, out, tabs, weights, GU, DW, w_loaded):
    tok, dst, slot_e, slot_buf, cum_i, turns = tabs
    with ExitStack() as ctx:
        sb = lambda n, s, d: ctx.enter_context(nc.sbuf_tensor(n, s, d))
        ps = lambda n, s: ctx.enter_context(nc.psum_tensor(n, s, F32))
        sem = lambda n: ctx.enter_context(nc.semaphore(n))

        gw = sb("gw", [P, C, E_], F32)
        mv = sb("r_mv", [P, NT, 2], F32)
        eps, std, rstd = sb("r_eps", [P, 1], F32), sb("r_std", [P, NT], F32), sb("r_rstd", [P, NT], F32)
        xn = [sb(f"r_xn{i}", [P, D], F32) for i in range(NX)]
        xnT = [sb(f"r_xnT{i}", [P, C, P], F32) for i in range(2)]
        lgT = [sb(f"lgT{i}", [E_, P], F32) for i in range(2)]
        lg = sb("lg", [P, NT, E_], F32)
        top, idx = sb("top", [P, NT, 8], F32), sb("idx", [P, NT, 8], U32)
        d4, e4 = sb("d4", [P, NT, K_], F32), sb("e4", [P, NT, K_], F32)
        s4, r4 = sb("s4", [P, NT, 1], F32), sb("r4", [P, NT, 1], F32)
        idf = sb("idf", [P, NT, K_], F32)
        w4 = sb("w4", [P, NT, K_], F32)
        wx = sb("wx", [P, NT, K_, E_], F32)
        wa, wb, wrow = (sb(n, [P, NT, E_], F32) for n in ("wa", "wb", "wrow"))
        zeros = sb("r_zeros", [P, D], F32)
        iota_e = sb("iota_e", [P, E_], F32)
        iota_j = sb("iota_j", [P, NT - 1], F32)
        iota_s = sb("iota_s", [P, NS], F32)
        iota_r = sb("iota_r", [P, P], F16)
        iota_q = sb("iota_q", [P, NS], F16)
        none = sb("none", [P, 1], F32)
        number = sb("number", [P, NT], F32)
        oh = sb("oh", [P, NT, K_, E_], F32)
        pr = sb("pr", [P, NT, K_, E_], F32)
        m1, m2 = sb("m1", [P, NT, E_], F32), sb("m2", [P, NT, E_], F32)
        mask = sb("mask", [P, NT, E_], BF16)
        upper = sb("upper", [P, P], BF16)
        ones = sb("ones", [P, P], BF16)
        cmp_n = sb("cmp_n", [P, E_, NT - 1], F32)
        n_e = sb("n_e", [P, E_], F32)
        sl, cum, base, zero = (sb(n, [P, E_], F32) for n in ("sl", "cum", "base", "zero"))
        pos = sb("pos", [P, NT, E_], F32)
        destf = sb("destf", [P, NT, K_], F32)
        qi, ri = sb("qi", [P, NT, K_], I32), sb("ri", [P, NT, K_], I32)
        qf, rf = sb("qf", [P, NT, K_], F32), sb("rf", [P, NT, K_], F32)
        desti = sb("desti", [P, NT, K_], I32)
        end_x, end = sb("end_x", [E_, E_], F32), sb("end", [E_, 1], F32)
        past = sb("past", [E_, NS], BF16)
        sef = sb("sef", [P, NS], F32)
        ohr, rown = ([sb(f"{n}{i}", [P, K_, P], F16) for i in range(2)] for n in ("ohr", "rown"))
        ohq = [sb(f"ohq{i}", [P, K_, NS], F16) for i in range(2)]
        more = sb("more", [P, 1], I32)
        tabf, empty, far = sb("tabf", [P, NS], F32), sb("empty", [P, NS], F32), sb("far", [P, NS], F32)

        xt_ps = [ps(f"r_xt{i}", [P, 512]) for i in range(2)]
        lgT_ps = [ps(f"r_lgT{i}", [P, 512]) for i in range(2)]
        lg_ps = ps("r_lg", [P, NT, E_])
        pos_ps, cnt_ps, tab_ps = ps("pos_ps", [P, NT, E_]), ps("cnt_ps", [P, 512]), ps("tab_ps", [P, 512])

        gw_loaded, iotas, tri = sem("gw_loaded"), sem("iotas"), sem("tri")
        step = sem("r_step")
        var_ready, std_ready = sem("r_var"), sem("r_std_ready")
        xn_ready, xn_stored = sem("r_xn"), [sem(f"r_stored{i}") for i in range(NX)]
        zeros_ready, out_ready, w_ready, w_stored = sem("zeros_ready"), sem("out_ready"), sem("w_ready"), sem("w_stored")
        ohr_ready, rown_ready, ohq_ready = sem("ohr_ready"), sem("rown_ready"), sem("ohq_ready")
        w4_ready, w_step, ends_ready, ends_full = sem("w4_ready"), sem("w_step"), sem("ends_ready"), sem("ends_full")
        xt_full, xt_empty, lgT_full, lgT_ready, lg_full = (
            sem("r_xtf"), sem("r_xte"), sem("r_lgtf"), sem("r_lgtr"), sem("r_lgf"))
        d4_ready, e4_ready = sem("d4_ready"), sem("e4_ready")
        mask_ready, pos_full, tab_clear, tab_used = (sem(n) for n in (
            "mask_ready", "pos_full", "tab_clear", "tab_used"))

        block = ctx.enter_context(nc.Block())

        @block.sync
        def _(sp):
            sp.dma_start(gw[:, :, :], gate_w).then_inc(gw_loaded, DMA)
            with sp.Fori(0, NT // NX) as i:
                for p in range(NX):
                    t = i * NX + p
                    sp.wait_ge(xn_ready, t + 1)
                    sp.dma_start(xd[bass.ds(t * P, P), 0:D], xn[p][:, :]).then_inc(xn_stored[p], DMA)
            sp.dma_start(out[0:NT * P, :].rearrange("(t p) d -> p t d", p=P), xs[:, :, :]).then_inc(out_ready, DMA)
            sp.wait_ge(zeros_ready, 1)
            sp.dma_start(out[NT * P:(NT + 1) * P, :], zeros[:, :]).then_inc(out_ready, DMA)
            load_expert(sp, weights, GU, DW, w_loaded, 0, 0)
            load_expert(sp, weights, GU, DW, w_loaded, 0, 1)
            sp.wait_ge(w_ready, 1)
            sp.dma_start(xd[:, D:D + E_].rearrange("(t p) e -> p t e", p=P), wrow[:, :, :]).then_inc(w_stored, DMA)
            for p in range(NX):
                sp.wait_ge(xn_stored[p], DMA * (NT // NX + 1))
            sp.wait_ge(w_stored, DMA)
            sp.wait_ge(out_ready, 2 * DMA)

        @block.gpsimd
        def _(pool):
            for p in range(NX):
                pool.sem_inc(xn_stored[p], DMA)
            pool.iota(iota_e[:, :], [[1, E_]], 0, 0, allow_small_or_imprecise_dtypes=True)
            pool.iota(iota_j[:, :], [[P, NT - 1]], P, 0, allow_small_or_imprecise_dtypes=True)
            pool.iota(iota_s[:, :], [[1, NS]], 0, 0, allow_small_or_imprecise_dtypes=True)
            pool.iota(iota_r[:, :], [[1, P]], 0, 0, allow_small_or_imprecise_dtypes=True)
            pool.iota(iota_q[:, :], [[1, NS]], 0, 0, allow_small_or_imprecise_dtypes=True)
            pool.iota(none[:, :], [[0, 1]], NT * P + 1, 1, allow_small_or_imprecise_dtypes=True)
            pool.iota(number[:, :], [[P, NT]], 1, 1, allow_small_or_imprecise_dtypes=True)
            pool.memset(zeros[:, :], 0.0).then_inc(zeros_ready, 1)
            pool.memset(zero[:, :], 0.0)
            pool.memset(ones[:, :], 1.0)
            pool.memset(upper[:, :], 1.0).then_inc(iotas, 1)
            pool.wait_ge(iotas, 1)
            pool.affine_select(out=upper[:, :], in_=upper[:, :], compare_op=ALU.is_gt, fill=0.0, base=0,
                               pattern=[[1, P]], channel_multiplier=-1).then_inc(tri, 1)
            pool.wait_ge(w4_ready, 1)
            for k in range(K_):
                m = pool.tensor_tensor(wx[:, :, k, :], oh[:, :, k, :], w4[:, :, k:k + 1].broadcast_to([P, NT, E_]),
                                       ALU.mult)
            m.then_inc(w_step, 1)
            pool.wait_ge(w_step, 1)
            pool.tensor_tensor(wa[:, :, :], wx[:, :, 0, :], wx[:, :, 1, :], ALU.add)
            pool.tensor_tensor(wb[:, :, :], wx[:, :, 2, :], wx[:, :, 3, :], ALU.add).then_inc(w_step, 1)
            pool.wait_ge(w_step, 2)
            pool.tensor_tensor(wrow[:, :, :], wa[:, :, :], wb[:, :, :], ALU.add).then_inc(w_ready, 1)

        @block.scalar
        def _(act):
            act.wait_ge(var_ready, 1)
            act.activation(std[:, :], mv[:, :, 1], ACT.Sqrt, bias=eps[:, :]).then_inc(std_ready, 1)
            with act.Fori(0, NT // 2) as i:
                for p in range(2):
                    t = i * 2 + p
                    act.wait_ge(xt_full, t + 1 + NX)
                    act.copy(xnT[p][:, :, :], xt_ps[p][:, :].rearrange("p (c t) -> p c t", c=C)).then_inc(xt_empty, 1)
            act.wait_ge(d4_ready, 1)
            act.activation(e4[:, :, :], d4[:, :, :], ACT.Exp).then_inc(e4_ready, 1)
            with act.Fori(0, NT // 2) as i:
                for p in range(2):
                    t = i * 2 + p
                    act.wait_ge(tab_used, t + 1)
                    act.wait_ge(ohr_ready, t + 1)
                    act.activation(rown[p][:, :, :], ohr[p][:, :, :], ACT.Copy,
                                   scale=number[:, bass.ds(t, 1)]).then_inc(rown_ready, 1)

        @block.tensor
        def _(pe):
            pe.sem_inc(xt_full, NX)
            pe.sem_inc(lg_full, 2)
            pe.wait_ge(gw_loaded, DMA)

            def transpose(t, p):
                pe.wait_ge(xn_ready, t + 1)
                if not (isinstance(t, int) and t < 2):
                    pe.wait_ge(xt_empty, t - 1)
                for c in range(C):
                    m = pe.transpose(xt_ps[p % 2][:, c * P:(c + 1) * P], xn[p][:, c * P:(c + 1) * P], ident[:, :])
                m.then_inc(xt_full, 1)

            def logits(t, p):
                pe.wait_ge(xt_empty, t + 1)
                pe.wait_ge(lgT_ready, t + 1)
                for c in range(C):
                    m = pe.matmul(lgT_ps[p][0:E_, 0:P], gw[:, c, :], xnT[p][:, c, :], start=(c == 0), stop=(c == C - 1))
                m.then_inc(lgT_full, 1)

            def turn_logits(t, p):
                pe.wait_ge(lgT_ready, t + 3)
                pe.matmul(lg_ps[:, bass.ds(t, 1), :].rearrange("p a e -> p (a e)"), lgT[p][:, :],
                          ident[0:E_, 0:E_], start=True, stop=True).then_inc(lg_full, 1)

            transpose(0, 0)
            transpose(1, 1)
            logits(0, 0)
            with pe.Fori(0, NT // NX - 1) as i:
                for p in range(NX):
                    transpose(i * NX + p + 2, (p + 2) % NX)
                    logits(i * NX + p + 1, (p + 1) % 2)
                    turn_logits(i * NX + p, p % 2)
            for t in range(NT - NX, NT):
                if t + 2 < NT:
                    transpose(t + 2, (t + 2) % NX)
                if t + 1 < NT:
                    logits(t + 1, (t + 1) % 2)
                turn_logits(t, t % 2)
            pe.wait_ge(tri, 1)
            pe.wait_ge(mask_ready, 1)
            pe.matmul(pos_ps[:, :, :], upper[:, :], mask[:, :, :], start=True, stop=True)
            for t in range(NT - 1):
                m = pe.matmul(pos_ps[:, t + 1:NT, :], ones[:, :],
                              mask[:, t:t + 1, :].broadcast_to([P, NT - 1 - t, E_]),
                              start=False, stop=True, skip_group_check=True)
            for t in range(NT):
                m = pe.matmul(cnt_ps[:, 0:E_], ones[:, :], mask[:, t, :], start=(t == 0), stop=(t == NT - 1))
            m.then_inc(pos_full, 1)
            pe.wait_ge(ends_ready, 1)
            pe.matmul(cnt_ps[:, E_:E_ + NS], ones[0:E_, :], past[:, :], start=True, stop=True).then_inc(ends_full, 1)
            pe.wait_ge(tab_clear, 1)
            with pe.Fori(0, NT // 2) as i:
                for p in range(2):
                    t = i * 2 + p
                    pe.wait_ge(rown_ready, t + 1)
                    pe.wait_ge(ohq_ready, t + 1)
                    for k in range(K_):
                        m = pe.matmul(tab_ps[:, 0:NS], rown[p][:, k, :], ohq[p][:, k, :], start=False, stop=True,
                                      skip_group_check=True)
                    m.then_inc(tab_used, 1)

        @block.vector
        def _(dve):
            made = [0]

            def done(ins):
                made[0] += 1
                ins.then_inc(step, 1)
                dve.wait_ge(step, made[0])

            dve.sem_inc(tab_used, 2)
            dve.sem_inc(lgT_ready, 2)
            dve.memset(eps[:, :], EPS)
            for t in range(NT):
                s = dve.bn_aggr(mv[:, t, :], st6[:, t, :])
            s.then_inc(var_ready, 1)
            dve.wait_ge(std_ready, 1)
            done(dve.reciprocal(rstd[:, :], std[:, :]))

            def normalise(t, p):
                dve.wait_ge(xt_full, t + 1)
                dve.wait_ge(xn_stored[p], (t - p) * (DMA // NX) + DMA)
                dve.tensor_scalar(xn[p][:, :], xs[:, bass.ds(t, 1), :].rearrange("p a d -> p (a d)"),
                                  mv[:, bass.ds(t, 1), 0], rstd[:, bass.ds(t, 1)], ALU.subtract,
                                  ALU.mult).then_inc(xn_ready, 1)

            def logits_evac(t, p):
                dve.wait_ge(lgT_full, t + 1)
                dve.wait_ge(lg_full, t + 1)
                dve.tensor_copy(lgT[p][:, :], lgT_ps[p][0:E_, 0:P]).then_inc(lgT_ready, 1)

            for p in range(NX - 1):
                normalise(p, p)
            with dve.Fori(0, NT // NX - 1) as i:
                for p in range(NX):
                    normalise(i * NX + p + NX - 1, (p + NX - 1) % NX)
                    logits_evac(i * NX + p, p % 2)
            normalise(NT - 1, NX - 1)
            for t in range(NT - NX, NT):
                logits_evac(t, t % 2)
            dve.wait_ge(lg_full, NT + 2)
            done(dve.tensor_copy(lg[:, :, :], lg_ps[:, :, :]))
            for t in range(NT):
                s = dve.max(top[:, t, :], lg[:, t, :])
            done(s)
            for t in range(NT):
                s = dve.max_index(idx[:, t, :], top[:, t, :], lg[:, t, :])
            done(s)
            dve.tensor_tensor(d4[:, :, :], top[:, :, 0:K_], top[:, :, 0:1].broadcast_to([P, NT, K_]),
                              ALU.subtract).then_inc(d4_ready, 1)
            done(dve.tensor_copy(idf[:, :, :], idx[:, :, 0:K_]))
            dve.wait_ge(iotas, 1)
            ie = iota_e[:, :].unsqueeze(1).broadcast_to([P, NT, E_])
            for k in range(K_):
                s = dve.tensor_tensor(oh[:, :, k, :], ie, idf[:, :, k:k + 1].broadcast_to([P, NT, E_]), ALU.is_equal)
            done(s)
            dve.tensor_tensor(m1[:, :, :], oh[:, :, 0, :], oh[:, :, 1, :], ALU.add)
            done(dve.tensor_tensor(m2[:, :, :], oh[:, :, 2, :], oh[:, :, 3, :], ALU.add))
            dve.tensor_tensor(mask[:, :, :], m1[:, :, :], m2[:, :, :], ALU.add).then_inc(mask_ready, 1)
            dve.wait_ge(e4_ready, 1)
            done(dve.tensor_reduce(s4[:, :, :], e4[:, :, :], AX.X, ALU.add))
            done(dve.reciprocal(r4[:, :, :], s4[:, :, :]))
            dve.tensor_tensor(w4[:, :, :], e4[:, :, :], r4[:, :, :].broadcast_to([P, NT, K_]),
                              ALU.mult).then_inc(w4_ready, 1)
            dve.wait_ge(pos_full, 1)
            done(dve.tensor_copy(n_e[:, :], cnt_ps[:, 0:E_]))
            done(dve.tensor_tensor(cmp_n[:, :, :], n_e[:, :].unsqueeze(2).broadcast_to([P, E_, NT - 1]),
                                   iota_j[:, :].unsqueeze(1).broadcast_to([P, E_, NT - 1]), ALU.is_gt))
            done(dve.tensor_reduce(sl[:, :], cmp_n[:, :, :], AX.X, ALU.add))
            done(dve.tensor_scalar(sl[:, :], sl[:, :], 1.0, None, ALU.add))
            done(dve.tensor_tensor_scan(cum[:, :], sl[:, :], zero[:, :], 0.0, ALU.add, ALU.add))
            done(dve.tensor_tensor(base[:, :], cum[:, :], sl[:, :], ALU.subtract))
            done(dve.tensor_tensor(end_x[:, :], cum[0:E_, :], ident[0:E_, 0:E_], ALU.mult))
            done(dve.tensor_reduce(end[:, :], end_x[:, :], AX.X, ALU.add))
            dve.tensor_scalar(past[:, :], iota_s[0:E_, :], end[:, :], None, ALU.is_ge).then_inc(ends_ready, 1)
            done(dve.tensor_scalar(base[:, :], base[:, :], float(TILE), None, ALU.mult))
            done(dve.tensor_copy(cum_i[:, :], cum[:, :]))
            done(dve.tensor_scalar(more[:, :], cum_i[:, E_ - 1:E_], 1, None, ALU.add))
            done(dve.tensor_scalar(turns[:, 0:1], more[:, :], 1, None, ALU.arith_shift_right))
            dve.tensor_scalar(turns[:, 1:2], turns[:, 0:1], 2, 2, ALU.mult, ALU.subtract)
            dve.memset(tok[:, NS:NS + 2], 0)
            dve.memset(slot_e[:, NS:NS + 2], 0)
            dve.memset(slot_buf[:, NS:NS + 2], 0)
            done(dve.tensor_tensor(pos[:, :, :], pos_ps[:, :, :], base[:, :].unsqueeze(1).broadcast_to([P, NT, E_]),
                                   ALU.add))
            for k in range(K_):
                s = dve.tensor_tensor(pr[:, :, k, :], oh[:, :, k, :], pos[:, :, :], ALU.mult)
            done(s)
            done(dve.tensor_reduce(destf[:, :, :], pr[:, :, :, :], AX.X, ALU.add))
            done(dve.tensor_copy(desti[:, :, :], destf[:, :, :]))
            dve.tensor_scalar(qi[:, :, :], desti[:, :, :], 7, None, ALU.arith_shift_right)
            done(dve.tensor_scalar(ri[:, :, :], desti[:, :, :], P - 1, None, ALU.bitwise_and))
            dve.tensor_copy(qf[:, :, :], qi[:, :, :])
            dve.memset(tab_ps[:, 0:NS], 0.0).then_inc(tab_clear, 1)
            done(dve.tensor_copy(rf[:, :, :], ri[:, :, :]))
            with dve.Fori(0, NT // 2) as i:
                for p in range(2):
                    t = i * 2 + p
                    dve.wait_ge(tab_used, t + 1)
                    r = rf[:, bass.ds(t, 1), :].rearrange("p a k -> p (a k)").unsqueeze(2).broadcast_to([P, K_, P])
                    dve.tensor_tensor(ohr[p][:, :, :], iota_r[:, :].unsqueeze(1).broadcast_to([P, K_, P]), r,
                                      ALU.is_equal).then_inc(ohr_ready, 1)
                    q = qf[:, bass.ds(t, 1), :].rearrange("p a k -> p (a k)").unsqueeze(2).broadcast_to([P, K_, NS])
                    dve.tensor_tensor(ohq[p][:, :, :], iota_q[:, :].unsqueeze(1).broadcast_to([P, K_, NS]), q,
                                      ALU.is_equal).then_inc(ohq_ready, 1)
            dve.wait_ge(ends_full, 1)
            done(dve.tensor_copy(sef[:, :], cnt_ps[:, E_:E_ + NS]))
            done(dve.tensor_scalar(sef[:, :], sef[:, :], float(E_ - 1), None, ALU.min))
            done(dve.tensor_copy(slot_e[:, 0:NS], sef[:, :]))
            dve.tensor_scalar(slot_buf[:, 0:NS], slot_e[:, 0:NS], NW - 1, None, ALU.bitwise_and)
            dve.wait_ge(tab_used, NT + 2)
            done(dve.tensor_copy(tabf[:, :], tab_ps[:, 0:NS]))
            done(dve.tensor_scalar(empty[:, :], tabf[:, :], 0.0, none[:, :], ALU.is_equal, ALU.mult))
            dve.tensor_scalar(tok[:, 0:NS], tabf[:, :], 1.0, 1.0, ALU.max, ALU.subtract)
            done(dve.tensor_tensor(far[:, :], tabf[:, :], empty[:, :], ALU.add))
            done(dve.tensor_scalar(dst[:, :], far[:, :], 1.0, None, ALU.subtract))


def experts(nc, ident, xd, out, tabs, weights, GU, DW, w_loaded):
    tok, dst, slot_e, slot_buf, cum_i, turns = tabs
    with ExitStack() as ctx:
        sb = lambda n, s, d: ctx.enter_context(nc.sbuf_tensor(n, s, d))
        ps = lambda n, s: ctx.enter_context(nc.psum_tensor(n, s, F32))
        sem = lambda n: ctx.enter_context(nc.semaphore(n))

        idx = [sb(f"gidx{i}", [P, 1], U32) for i in range(2)]
        yidx = [sb(f"yidx{i}", [P, 1], U32) for i in range(2)]
        xg = [sb(f"xg{i}", [P, XW], F32) for i in range(2)]
        wt = [sb(f"wt{i}", [P, 1], F32) for i in range(2)]
        xT = [sb(f"xT{i}", [P, C, P], F32) for i in range(2)]
        sg = [sb(f"sg{i}", [P, IW], F32) for i in range(2)]
        a = [sb(f"a{i}", [P, IW], F32) for i in range(2)]
        aT = [sb(f"aT{i}", [P, 3, P], F32) for i in range(2)]
        yb = [sb(f"yb{i}", [P, D], F32) for i in range(2)]

        xt_ps = [ps(f"xt_ps{i}", [P, 512]) for i in range(2)]
        g_ps = [ps(f"g_ps{i}", [P, 512]) for i in range(2)]
        u_ps = [ps(f"u_ps{i}", [P, 512]) for i in range(2)]
        at_ps, y_ps = ps("at_ps", [P, 4, P]), ps("y_ps", [P, D])

        experts_ready, slots_done = sem("experts_ready"), sem("slots_done")
        idx_ready, x_loaded = sem("idx_ready"), [sem(f"xg_loaded{i}") for i in range(2)]
        xt_full, xt_empty, gu_full = sem("xt_full2"), sem("xt_empty2"), sem("gu_full")
        wt_ready = sem("wt_ready")
        sg_ready, a_ready, at_full, at_empty = sem("sg_ready"), sem("a_ready"), sem("at_full"), sem("at_empty")
        y_empty, y_added, yi_ready = sem("y_empty"), sem("y_added"), sem("yi_ready")
        passed = sem("e_passed")

        block = ctx.enter_context(nc.Block())

        @block.sync
        def _(sp):
            def arrived(i, p):
                sp.wait_ge(w_loaded[p], i * 5 * DMA + 5 * DMA)
                sp.sem_inc(experts_ready, 1)

            arrived(0, 0)
            arrived(0, 1)
            with sp.Fori(1, E_ // 2) as i:
                for p in range(2):
                    last = sp.value_load(cum_i[0:1, bass.ds(i * 2 + p - 2, 1)], min_val=1, max_val=NS)
                    sp.wait_ge(slots_done, last)
                    load_expert(sp, weights, GU, DW, w_loaded, i, p)
                    arrived(i, p)

        def count(eng):
            return (eng.value_load(turns[0:1, 0:1], min_val=E_ // 2, max_val=NS // 2),
                    eng.value_load(turns[0:1, 1:2], min_val=E_ - 2, max_val=NS - 2))

        @block.gpsimd
        def _(pool):
            def gather(s, p):
                if not (isinstance(s, int) and s < 2):
                    pool.wait_ge(xt_full, s - 1)
                    pool.wait_ge(wt_ready, s - 1)
                pool.tensor_copy(idx[p][:, :], tok[:, bass.ds(s, 1)]).then_inc(idx_ready, 1)
                pool.wait_ge(idx_ready, s + 1)
                pool.sem_inc(passed, 1)
                pool.indirect_dma_start(xg[p][:, :], None, xd[:, :], bass.IndirectOffsetOnAxis(idx[p][:, :], 0))\
                    .then_inc(x_loaded[p], DMA)

            def add(s, p):
                pool.tensor_copy(yidx[p][:, :], dst[:, bass.ds(s, 1)]).then_inc(yi_ready, 1)
                pool.wait_ge(yi_ready, s + 1)
                pool.sem_inc(passed, 1)
                pool.wait_ge(y_empty, s + 1)
                pool.sem_inc(passed, 1)
                if not (isinstance(s, int) and s == 0):
                    pool.wait_ge(y_added, s * DMA)
                    pool.sem_inc(passed, 1)
                pool.indirect_dma_start(out[:, :], bass.IndirectOffsetOnAxis(yidx[p][:, :], 0), yb[p][:, :], None,
                                        compute_op=ALU.add).then_inc(y_added, DMA)

            for s in range(4):
                gather(s, s % 2)
            add(0, 0)
            n, last = count(pool)
            with pool.Fori(1, NS // 2) as i:
                with pool.If(i < n):
                    for p in range(2):
                        gather(i * 2 + p + 2, p)
                        add(i * 2 + p - 1, 1 - p)
            add(last + 1, 1)
            pool.wait_ge(y_added, last * DMA + 2 * DMA)
            for p in range(2):
                pool.wait_ge(x_loaded[p], n * DMA + DMA)

        @block.scalar
        def _(act):
            def x_evac(s, p):
                act.wait_ge(xt_full, s + 1)
                act.copy(xT[p][:, :, :], xt_ps[p][:, :].rearrange("p (c t) -> p c t", c=C)).then_inc(xt_empty, 1)

            def silu(s, p):
                act.wait_ge(gu_full, s + 1)
                act.activation(sg[p][:, :], g_ps[p][:, 0:IW], ACT.Silu).then_inc(sg_ready, 1)

            def y_evac(s, p):
                act.wait_ge(slots_done, s + 1)
                act.wait_ge(wt_ready, s + 1)
                if not (isinstance(s, int) and s < 2):
                    act.wait_ge(y_added, (s - 1) * DMA)
                act.activation(yb[p][:, :], y_ps[:, :], ACT.Copy, scale=wt[p][:, :]).then_inc(y_empty, 1)

            def slot(s, p, first=False):
                silu(s, p)
                x_evac(s + 1, 1 - p)
                if not first:
                    y_evac(s - 1, 1 - p)

            x_evac(0, 0)
            slot(0, 0, first=True)
            slot(1, 1)
            n, last = count(act)
            with act.Fori(1, NS // 2) as i:
                with act.If(i < n):
                    slot(i * 2, 0)
                    slot(i * 2 + 1, 1)
            y_evac(last + 1, 1)

        @block.vector
        def _(dve):
            def at_evac(s, p):
                dve.wait_ge(at_full, s + 1)
                dve.tensor_copy(aT[p][:, 0::2, :], at_ps[:, 0:3:2, :])
                dve.tensor_copy(aT[p][0:IL - P, 1, :], at_ps[0:IL - P, 1, :]).then_inc(at_empty, 1)

            def weights_of(s, p):
                e = dve.value_load(slot_e[0:1, bass.ds(s, 1)], min_val=0, max_val=E_ - 1)
                dve.wait_ge(x_loaded[p], (s - p) * (DMA // 2) + DMA)
                if not (isinstance(s, int) and s < 2):
                    dve.wait_ge(y_empty, s - 1)
                dve.tensor_copy(wt[p][:, :], xg[p][:, bass.ds(e + D, 1)]).then_inc(wt_ready, 1)

            def gated(s, p):
                weights_of(s, p)
                dve.wait_ge(sg_ready, s + 1)
                dve.tensor_tensor(a[p][:, 0:IL], u_ps[p][:, 0:IL], sg[p][:, 0:IL], ALU.mult)
                dve.scalar_tensor_tensor(a[p][:, IL:IW], u_ps[p][:, IL:IW], SMALL, sg[p][:, IL:IW], ALU.mult,
                                         ALU.mult).then_inc(a_ready, 1)

            gated(0, 0)
            at_evac(0, 0)
            gated(1, 1)
            n, last = count(dve)
            with dve.Fori(1, NS // 2) as i:
                with dve.If(i < n):
                    for p in range(2):
                        at_evac(i * 2 + p - 1, 1 - p)
                        gated(i * 2 + p, p)
            at_evac(last + 1, 1)

        @block.tensor
        def _(pe):
            def transpose_x(s, p):
                pe.wait_ge(x_loaded[p], (s - p) * (DMA // 2) + DMA)
                for c in range(C):
                    m = pe.transpose(xt_ps[p][:, c * P:(c + 1) * P], xg[p][:, c * P:(c + 1) * P], ident[:, :])
                m.then_inc(xt_full, 1)

            def gate_up(s, p, buf):
                pe.wait_ge(xt_empty, s + 1)
                for ps_, g in ((g_ps, 0), (u_ps, 1)):
                    for c in range(C):
                        m = pe.matmul(ps_[p][:, 0:IW], xT[p][:, c, :],
                                      GU[:, bass.ds(buf, 1), c, g, :].rearrange("p a f -> p (a f)"),
                                      start=(c == 0), stop=(c == C - 1))
                m.then_inc(gu_full, 1)

            def transpose_a(s, p):
                pe.wait_ge(a_ready, s + 1)
                pe.transpose(at_ps[:, 0, :], a[p][:, 0:P], ident[:, :])
                pe.transpose(at_ps[0:IL - P, 1, :], a[p][:, P:IL], ident[:, :])
                pe.transpose(at_ps[:, 2, :], a[p][:, IL:IW], ident[:, :]).then_inc(at_full, 1)

            def down(s, p, buf):
                pe.wait_ge(at_empty, s + 1)
                if not (isinstance(s, int) and s == 0):
                    pe.wait_ge(y_empty, s)
                for c in range(3):
                    rows = slice(0, IL - P) if c == 1 else slice(0, P)
                    m = pe.matmul(y_ps[:, :], aT[p][rows, c, :],
                                  DW[rows, bass.ds(buf, 1), c, :].rearrange("p a d -> p (a d)"),
                                  start=(c == 0), stop=(c == 2))
                m.then_inc(slots_done, 1)

            def slot(s, p, first=False):
                e = pe.value_load(slot_e[0:1, bass.ds(s, 1)], min_val=0, max_val=E_ - 1)
                buf = pe.value_load(slot_buf[0:1, bass.ds(s, 1)], min_val=0, max_val=NW - 1)
                if not first:
                    transpose_a(s - 1, 1 - p)
                pe.wait_ge(experts_ready, e + 1)
                gate_up(s, p, buf)
                transpose_x(s + 1, 1 - p)
                if not first:
                    down(s - 1, 1 - p, pe.value_load(slot_buf[0:1, bass.ds(s - 1, 1)], min_val=0, max_val=NW - 1))

            transpose_x(0, 0)
            slot(0, 0, first=True)
            slot(1, 1)
            n, last = count(pe)
            with pe.Fori(1, NS // 2) as i:
                with pe.If(i < n):
                    slot(i * 2, 0)
                    slot(i * 2 + 1, 1)
            transpose_a(last + 1, 1)
            down(last + 1, 1, pe.value_load(slot_buf[0:1, bass.ds(last + 1, 1)], min_val=0, max_val=NW - 1))


def build(nc, t, out):
    qd = nc.dram_tensor("qd", (NB, 3, P, C * S), BF16, kind="Internal").ap()
    kd = nc.dram_tensor("kd", (NB, 3, P, S), BF16, kind="Internal").ap()
    md = nc.dram_tensor("md", (NB, J // CH, 3, 2 * CH, S), BF16, kind="Internal").ap()
    xd = nc.dram_tensor("xd", (NT * P, XW), F32, kind="Internal").ap()
    with ExitStack() as ctx:
        sb = lambda n, s, d: ctx.enter_context(nc.sbuf_tensor(n, s, d))
        xs, ident = sb("xs", [P, NT, D], F32), sb("ident", [P, P], F32)
        st_new = sb("st_new", [P, NT, 6], F32)
        GU = sb("GU", [P, NW, C, 2, IW], F32)
        DW = sb("DW", [P, NW, 3, D], F32)
        tabs = (sb("tok", [P, NS + 2], U32), sb("dst", [P, NS], U32), sb("slot_e", [P, NS + 2], I32),
                sb("slot_buf", [P, NS + 2], I32), sb("cum_i", [P, E_], I32), sb("turns", [P, 2], I32))
        w_loaded = [ctx.enter_context(nc.semaphore(f"w_loaded{i}")) for i in range(NW)]
        weights = (t["wgu_l"], t["wgu_s"], t["wd_l"], t["wd_s"])
        attention(nc, t["x"], t["ctx"], t["wq"], t["wk"], t["wv"], t["wfc"], t["bfc"], xs, st_new, ident, qd, kd, md)
        route(nc, t["gate_w"], xs, st_new, ident, xd, out, tabs, weights, GU, DW, w_loaded)
        experts(nc, ident, xd, out, tabs, weights, GU, DW, w_loaded)


def kernel(**inputs):
    import numpy as np
    import concourse.bacc as bacc
    from concourse.bass_utils import run_bass_kernel_spmd

    a = {k: np.asarray(v) for k, v in inputs.items()}
    order = np.arange(D).reshape(G, C, DH).transpose(1, 2, 0).reshape(-1)
    order_k = np.arange(P).reshape(G, DH).T.reshape(-1)

    def rows_in(w):
        return w.reshape(C, P, -1).transpose(1, 0, 2)

    def gate_up(g, u):
        n, _, f = g.shape
        return np.stack([g, u], 1).reshape(n, 2, C, P, f).transpose(0, 3, 2, 1, 4).reshape(n, P, 2 * C, f)

    arrays = {
        "x": a["x"].reshape(NT * P, D),
        "ctx": a["ctx_2048"].transpose(0, 2, 1).reshape(NB, C, P, S).transpose(0, 2, 1, 3),
        "wq": rows_in(a["L0_xattn_Wq"].T[:, order]),
        "wk": rows_in(a["L0_xattn_Wk"].T[:, order_k]),
        "wv": rows_in(a["L0_xattn_Wv"].T),
        "wfc": rows_in(a["L0_xattn_Wfc"].T),
        "bfc": np.broadcast_to(a["L0_xattn_bfc"], (P, D)),
        "gate_w": rows_in(a["L0_ffn_gate_w"].T),
        "wgu_l": gate_up(a["L0_ffn_Wg"], a["L0_ffn_Wu"]),
        "wgu_s": gate_up(a["L0_ffn_cWg"], a["L0_ffn_cWu"]),
        "wd_l": a["L0_ffn_Wd"],
        "wd_s": a["L0_ffn_cWd"],
    }
    arrays = {f"in_{k}": np.ascontiguousarray(v) for k, v in arrays.items()}
    nc = bacc.Bacc("TRN2", target_bir_lowering=False, num_devices=1)
    t = {k[3:]: nc.dram_tensor(k, v.shape, F32, kind="ExternalInput").ap() for k, v in arrays.items()}
    out = nc.dram_tensor("out_x", ((NT + 1) * P, D), F32, kind="ExternalOutput").ap()
    build(nc, t, out)
    r = run_bass_kernel_spmd(nc, [arrays], core_ids=[0])
    return r.results[0]["out_x"][:NT * P].reshape(NB, S, D)
```
